# Optimizing a Trainium2 kernel written in Bass

```python
import numpy as np
import jax
import jax.numpy as jnp

def _softmax(x, axis=-1):
    return jax.nn.softmax(x, axis=axis)

def _gelu(x):
    return jax.nn.gelu(x, approximate=True)

def _silu(x):
    return jax.nn.silu(x)

def _sigmoid(x):
    return jax.nn.sigmoid(x)

def _layernorm(x, axis=-1, eps=1e-05):
    m = jnp.mean(x, axis=axis, keepdims=True)
    v = jnp.var(x, axis=axis, keepdims=True)
    return (x - m) / jnp.sqrt(v + eps)

def _scatter_add(tgt, idx, src, axis=0):
    return tgt.at[idx].add(src)

def _segment_sum(src, seg, n):
    return jax.ops.segment_sum(src, seg, n)
kernel_name = 'mk_xattn_ffn_d1_seqx_r2_9d4f6c'

def setup_inputs(seed: int=0):
    np.random.seed(seed)
    _w = jnp.asarray

    def _rec_inputs():
        import jax
        import jax.numpy as jnp
        _rk = jax.random.key(seed)
        x = -0.0002928 + 1 * jax.random.normal(jax.random.fold_in(_rk, 1), (2, 2048, 512), jnp.float32)
        _lenS = 2048 - jax.random.randint(jax.random.fold_in(_rk, 7), (2,), 0, max(1, 2048 // 4) + 1, jnp.int32)
        _lenS2 = 128 - jax.random.randint(jax.random.fold_in(_rk, 8), (2,), 0, max(1, 128 // 4) + 1, jnp.int32)
        _ctx_1024P = jax.random.normal(jax.random.fold_in(_rk, 11), (2, 16, 512), jnp.float32)
        _ctx_1024c = jax.random.dirichlet(jax.random.fold_in(_rk, 511), 0.3 * jnp.ones((16,), jnp.float32), (2, 128))
        _ctx_1024t = jnp.einsum('bsk,bkd->bsd', _ctx_1024c, _ctx_1024P)
        _ctx_1024t = _ctx_1024t * jax.lax.rsqrt(jnp.mean(jnp.square(_ctx_1024t)) + 1e-12) * 0.953939
        ctx_1024 = -1.39393e-06 + 0.999914 * (_ctx_1024t + 0.3 * jax.random.normal(jax.random.fold_in(_rk, 611), (2, 128, 512), jnp.float32))
        _validS = jnp.arange(2048)[None, :] < _lenS[:, None]
        _validS2 = jnp.arange(128)[None, :] < _lenS2[:, None]
        _causal = jnp.tril(jnp.ones((2048, 2048), dtype=bool))
        mask_Bx1xSxS2_ik0 = jnp.where(jnp.broadcast_to(_validS2[:, None, None, :], (2, 1, 2048, 128)), 0, 1).astype(jnp.int32)
        return (x, ctx_1024, mask_Bx1xSxS2_ik0)
    x, ctx_1024, mask_Bx1xSxS2_ik0 = _rec_inputs()

    def _L0_xattn_setup():
        import jax, jax.numpy as jnp
        import numpy as np
        import math
        B, S, D, H = (2, 1024, 512, 16)
        DK = D // H
        key = jax.random.key(seed)
        ks = jax.random.split(key, 12)
        s = 1.0 / math.sqrt(D)
        inp = {'q': jax.random.normal(ks[0], (B, S, D), jnp.float32), 'k': jax.random.normal(ks[1], (B, S, D), jnp.float32), 'v': jax.random.normal(ks[2], (B, S, D), jnp.float32), 'mask': jnp.broadcast_to(jnp.tril(jnp.ones((S, S), jnp.int32))[None, None], (B, 1, S, S)), 'Wq': jax.random.normal(ks[3], (D, D), jnp.float32) * s, 'bq': jnp.zeros((D,), jnp.float32), 'Wk': jax.random.normal(ks[4], (D, D), jnp.float32) * s, 'bk': jnp.zeros((D,), jnp.float32), 'Wv': jax.random.normal(ks[5], (D, D), jnp.float32) * s, 'bv': jnp.zeros((D,), jnp.float32), 'Wo': jax.random.normal(ks[6], (D, D), jnp.float32) * s, 'bo': jnp.zeros((D,), jnp.float32)}
        return inp
    _L0_xattn_all = _L0_xattn_setup()
    _L0_xattn_in = {k: v for k, v in _L0_xattn_all.items() if k in ('Wq', 'bq', 'Wk', 'bk', 'Wv', 'bv', 'Wo', 'bo')}
    del _L0_xattn_all

    def _L0_ffn_setup():
        import jax, jax.numpy as jnp
        import numpy as np
        HIDDEN = 512
        INTER = 2048
        key = jax.random.key(seed)
        k1, k2, k3, k4, k5 = jax.random.split(key, 5)
        hidden_states = jax.random.normal(k1, (4, 1024, HIDDEN), dtype=jnp.float32)
        W1 = jax.random.normal(k2, (HIDDEN, INTER), dtype=jnp.float32) * (1.0 / np.sqrt(HIDDEN))
        b1 = jax.random.normal(k3, (INTER,), dtype=jnp.float32) * 0.02
        W2 = jax.random.normal(k4, (INTER, HIDDEN), dtype=jnp.float32) * (1.0 / np.sqrt(INTER))
        b2 = jax.random.normal(k5, (HIDDEN,), dtype=jnp.float32) * 0.02
        return {'hidden_states': hidden_states, 'W1': W1, 'b1': b1, 'W2': W2, 'b2': b2}
    _L0_ffn_all = _L0_ffn_setup()
    _L0_ffn_in = {k: v for k, v in _L0_ffn_all.items() if k in ('W1', 'b1', 'W2', 'b2')}
    del _L0_ffn_all
    return {'x': x, 'ctx_1024': ctx_1024, 'mask_Bx1xSxS2_ik0': mask_Bx1xSxS2_ik0, 'L0_xattn_Wq': _L0_xattn_in['Wq'], 'L0_xattn_bq': _L0_xattn_in['bq'], 'L0_xattn_Wk': _L0_xattn_in['Wk'], 'L0_xattn_bk': _L0_xattn_in['bk'], 'L0_xattn_Wv': _L0_xattn_in['Wv'], 'L0_xattn_bv': _L0_xattn_in['bv'], 'L0_xattn_Wo': _L0_xattn_in['Wo'], 'L0_xattn_bo': _L0_xattn_in['bo'], 'L0_ffn_W1': _L0_ffn_in['W1'], 'L0_ffn_b1': _L0_ffn_in['b1'], 'L0_ffn_W2': _L0_ffn_in['W2'], 'L0_ffn_b2': _L0_ffn_in['b2']}

def reference(x, ctx_1024, mask_Bx1xSxS2_ik0, L0_xattn_Wq, L0_xattn_bq, L0_xattn_Wk, L0_xattn_bk, L0_xattn_Wv, L0_xattn_bv, L0_xattn_Wo, L0_xattn_bo, L0_ffn_W1, L0_ffn_b1, L0_ffn_W2, L0_ffn_b2):
    import jax
    import jax.numpy as jnp

    def _L0_xattn_ref(q, k, v, mask, Wq, bq, Wk, bk, Wv, bv, Wo, bo):
        import jax, jax.numpy as jnp
        import numpy as np
        import math
        B, S, D, H = (2, 1024, 512, 16)
        DK = D // H
        b = q.shape[0]

        def heads(x, W, bias):
            y = x @ W.T + bias
            return y.reshape(b, -1, H, DK).transpose(0, 2, 1, 3)
        qh = heads(q, Wq, bq)
        kh = heads(k, Wk, bk)
        vh = heads(v, Wv, bv)
        scores = jnp.einsum('bhqd,bhkd->bhqk', qh, kh) / math.sqrt(DK)
        scores = jnp.where(mask == 0, jnp.float32(-1000000000.0), scores)
        weights = jax.nn.softmax(scores, axis=-1)
        out = jnp.einsum('bhqk,bhkd->bhqd', weights, vh)
        out = out.transpose(0, 2, 1, 3).reshape(b, -1, H * DK)
        return out @ Wo.T + bo

    def _L0_ffn_ref(hidden_states, W1, b1, W2, b2):
        import jax, jax.numpy as jnp
        import numpy as np
        HIDDEN = 512
        INTER = 2048
        h = jax.nn.relu(jnp.einsum('bsh,hi->bsi', hidden_states, W1) + b1)
        return jnp.einsum('bsi,ih->bsh', h, W2) + b2
    x = x + _L0_xattn_ref(_layernorm(x, axis=-1), ctx_1024, ctx_1024, mask_Bx1xSxS2_ik0, L0_xattn_Wq, L0_xattn_bq, L0_xattn_Wk, L0_xattn_bk, L0_xattn_Wv, L0_xattn_bv, L0_xattn_Wo, L0_xattn_bo)
    x = x + _L0_ffn_ref(_layernorm(x, axis=-1), L0_ffn_W1, L0_ffn_b1, L0_ffn_W2, L0_ffn_b2)
    return x

_drawn_inputs = setup_inputs


def setup_inputs(seed=0):
    import zlib

    import numpy as np

    out = dict(_drawn_inputs(seed))
    spreads = {'L0_xattn_bq': (0.0, 0.412),
     'L0_xattn_bk': (0.0, 0.8),
     'L0_xattn_bv': (0.0, 0.1),
     'L0_xattn_bo': (0.0, 0.1)}
    factors = {'L0_ffn_b1': 5.444, 'L0_ffn_b2': 3.925}
    for name, (base, spread) in spreads.items():
        noise = np.random.default_rng([zlib.crc32(name.encode()), seed]).standard_normal(out[name].shape)
        drawn = base * np.exp(spread * noise) if base else spread * noise
        out[name] = jnp.asarray(drawn.astype(out[name].dtype))
    for name, factor in factors.items():
        out[name] = (out[name] * factor).astype(out[name].dtype)
    return out
```

```python
from contextlib import ExitStack

import concourse.bass as bass
from concourse import mybir

F32 = mybir.dt.float32
F32R = mybir.dt.float32r
I32 = mybir.dt.int32
ALU = mybir.AluOpType
ACT = mybir.ActivationFunctionType
AX = mybir.AxisListType

P = 128
B = 2
S = 2048
D = 512
KEYS = 128
H = 16
DK = D // H
INTER = 2048
BLOCK = 512
TILES = BLOCK // P
NB = B * S // BLOCK
PAIRS = NB // B
KC = D // P
GROUPS = H // 4
UNITS = GROUPS * TILES
MC = INTER // P
LAG = 3
STAGE = 4
EPS = 1e-5
MASKED = -1000000000.0

JOBS = [(1, "q", 1), (4, "q", 2), (5, "o", 0), (6, "o", 1), (7, "o", 2), (8, "o", 3), (10, "q", 3),
        (11, "x", 0), (11, "x", 1), (12, "x", 2), (12, "x", 3), (14, "q0", 0)]
PV_SLOTS = {3: 3, 9: 0, 11: 1, 15: 2}
STATS_SLOTS = {0: 0, 1: 1, 2: 2, 3: 3}
APPLY_SLOTS = {7: 0, 8: 1, 9: 2, 10: 3}
RESIDUAL_SLOTS = {10: 0, 11: 1, 13: 2, 14: 3}
RSTD_SLOT = 5
KV_STEPS = 1 + GROUPS + 4 + 4 + B
N_PRO = TILES + 1


class Block:

    def __init__(self, i, b, first=False, last=False):
        self.i, self.b, self.first, self.last = i, b, first, last

    def at(self, per, k=0):
        return self.i * (2 * per) + (self.b * per + k)

    def jobs(self, slot=None):
        out, j, h = [], 0, 0
        for s, kind, which in JOBS:
            if (kind == "o" and self.first) or (kind == "q0" and self.last):
                continue
            if slot is None or s == slot:
                job = N_PRO + j if self.first else self.at(len(JOBS), N_PRO - TILES + j)
                out.append((kind, which, job, self.at(len(JOBS) - TILES, N_PRO + h)))
            j += 1
            h += kind != "o"
        return out

    def job(self, kind, which=0):
        return next(x[2] for x in self.jobs() if x[:2] == (kind, which))

    def q_ready(self, c):
        if c:
            return self.job("q", c) + 1
        return N_PRO if self.first else self.at(len(JOBS), N_PRO - TILES)

    def bank(self, kind, which):
        j = 0
        for _, k, w in JOBS:
            if (k, w) == (kind, which):
                break
            j += not (k == "o" and self.first)
        return (1 + j) % 2


JOBS_A = N_PRO + len(JOBS) * NB - TILES - 1
O_LAST = JOBS_A
FFN_JOB = JOBS_A + TILES
FFN_HI = N_PRO + (len(JOBS) - TILES) * NB - 1


def wait(eng, sem, value):
    if not isinstance(value, int) or value > 0:
        eng.wait_ge(sem, value)


def build(nc, x, ctxT, mask, wqT, bq, wkT, bk, wvT, bv, woT, bo, w1, b1, w2, b2, x2_dram, out):
    ctx = ExitStack()
    with ctx:
        base = -(-nc.sbuf_base // 64) * 64
        top = [base]

        def sb(name, shape, dt=F32, at=None):
            size = 4
            for n in shape[1:]:
                size *= n
            where = top[0] if at is None else at
            if at is None:
                top[0] += -(-size // 64) * 64
            t = nc.alloc_sbuf_tensor_at(name, shape, dt, offset=where)
            return t

        ident = sb("ident", [P, P])
        minus_half = sb("minus_half", [P, TILES])
        eps = sb("eps", [P, TILES])
        bo_row = sb("bo_row", [P, D])
        b2_row = sb("b2_row", [P, D])
        bq_col = sb("bq_col", [P, KC])
        bk_col = sb("bk_col", [P, KC])
        b1_col = sb("b1_col", [P, MC])
        stats = sb("stats", [P, TILES, 6])
        mean_var = sb("mean_var", [P, TILES, 2])
        rstd = sb("rstd", [P, TILES])
        neg_max = sb("neg_max", [P, TILES, 4])
        row_sum = sb("row_sum", [P, TILES, 4])
        row_inv = sb("row_inv", [P, TILES, 4])
        xn = sb("xn", [P, TILES, D])
        res = sb("res", [P, TILES, D])
        xT_hi = sb("xT_hi", [P, KC, BLOCK], F32R)
        xT_lo = sb("xT_lo", [P, KC, BLOCK], F32R)
        h_raw = sb("h_raw", [P, 2, BLOCK])
        h_hi = sb("h_hi", [P, 2, BLOCK], F32R)
        h_lo = sb("h_lo", [P, 2, BLOCK], F32R)
        stage_at = top[0]
        w_stage = sb("w_stage", [P, STAGE, 2, D])
        ffn_at = top[0]
        kbd_hi = sb("kbd_hi", [P, B, GROUPS, 4 * KEYS], F32R)
        kbd_lo = sb("kbd_lo", [P, B, GROUPS, 4 * KEYS], F32R)
        wq_hi = sb("wq_hi", [P, KC, D], F32R)
        wq_lo = sb("wq_lo", [P, KC, D], F32R)
        qT_hi = sb("qT_hi", [P, 2, BLOCK], F32R)
        qT_lo = sb("qT_lo", [P, 2, BLOCK], F32R)
        early_free = top[0]
        wo_hi = sb("wo_hi", [P, KC, D], F32R)
        wo_lo = sb("wo_lo", [P, KC, D], F32R)
        v_sb = sb("v_sb", [P, B, D])
        oT_at = top[0]
        oT_hi = sb("oT_hi", [P, GROUPS, BLOCK], F32R)
        oT_lo = sb("oT_lo", [P, GROUPS, BLOCK], F32R)
        sc = sb("sc", [P, TILES, 4, KEYS])
        pr = sb("pr", [P, TILES, 4, KEYS])
        pT_at = top[0]
        pT = sb("pT", [P, 2, 4, BLOCK])
        mask_sb = sb("mask_sb", [P, 2, TILES, KEYS], I32)
        end_a = top[0]
        chunk_bytes = 4 * D * 4
        early_chunks = (early_free - ffn_at) // chunk_bytes
        w_chunk = [sb(f"w_chunk{m}", [P, 4, D], F32R, at=ffn_at + m * chunk_bytes) for m in range(MC)]
        assert max(end_a, ffn_at + MC * chunk_bytes) <= nc.sbuf_usable_end
        wq_raw = sb("wq_raw", [P, KC, D], at=stage_at)
        wo_raw = sb("wo_raw", [P, KC, D], at=stage_at + 4 * KC * D)
        wk_raw = sb("wk_raw", [P, KC, D], at=pT_at)
        wv_raw = sb("wv_raw", [P, KC, D], at=pT_at + 4 * KC * D)
        ctx_raw = sb("ctx_raw", [P, KC, B * KEYS], at=oT_at)
        k_raw = sb("k_raw", [P, GROUPS, B, KEYS], at=oT_at + 4 * KC * B * KEYS)
        bv_row = sb("bv_row", [P, D], at=oT_at + 8 * KC * B * KEYS)

        bank = [ctx.enter_context(nc.psum_tensor(f"bank{n}", [P, 512], F32)) for n in range(8)]
        S_BANK, T_BANK, PV_BANK, JOB_BANK = bank[0:2], bank[2:4], bank[4:6], bank[6:8]
        UP_BANK, ACC_BANK = bank[0:2], bank[2:6]

        def sem(name):
            return ctx.enter_context(nc.semaphore(name))

        in_x = [sem(f"in_x{t}") for t in range(TILES)]
        in_res = [sem(f"in_res{t}") for t in range(TILES)]
        stored = [sem(f"stored{t}") for t in range(TILES)]
        in_mask = [sem(f"in_mask{b}") for b in range(B)]
        in_k, in_v, in_wq, in_wo = sem("in_k"), sem("in_v"), sem("in_wq"), sem("in_wo")
        in_rows, in_cols = sem("in_rows"), sem("in_cols")
        in_w = [sem(f"in_w{r}") for r in range(STAGE)]
        k_done, v_done = sem("k_done"), sem("v_done")
        scored = sem("scored")
        turned = sem("turned")
        pv_done = sem("pv_done")
        job_done = sem("job_done")
        up_done = sem("up_done")
        down_done = sem("down_done")
        exped = sem("exped")
        pT_ready = sem("pT_ready")
        job_hi = sem("job_hi")
        oT_hi_done = sem("oT_hi_done")
        relued = sem("relued")
        kv_step = sem("kv_step")
        wq_step = sem("wq_step")
        masked = sem("masked")
        maxed = sem("maxed")
        inverted = sem("inverted")
        job_out = sem("job_out")
        oT_ready = sem("oT_ready")
        counted = sem("counted")
        meaned = sem("meaned")
        normed = sem("normed")
        hi_done = sem("hi_done")
        h_ready = sem("h_ready")
        summed = sem("summed")
        passed = sem("passed")
        zeroed = sem("zeroed")
        made = sem("made")
        filled = sem("filled")
        scaled = sem("scaled")
        eps_added = sem("eps_added")
        rstd_ready = sem("rstd_ready")
        biased = sem("biased")
        wo_step = sem("wo_step")
        w_step = sem("w_step")

        x_v = x.rearrange("(b i t p) d -> b i t p d", b=B, i=PAIRS, t=TILES)
        mask_v = mask.rearrange("(b i t p) k -> b i p t k", b=B, i=PAIRS, t=TILES)
        x2_v = x2_dram.rearrange("(b i t p) d -> b i t p d", b=B, i=PAIRS, t=TILES)
        x2_n = x2_dram.rearrange("(n t p) d -> n t p d", n=NB, t=TILES)
        out_n = out.rearrange("(n t p) d -> n t p d", n=NB, t=TILES)
        w1_v = w1.rearrange("(k p) (m j) -> m p k j", p=P, j=P)
        w2_v = w2.rearrange("(m p) d -> m p d", p=P)

        def rows(w):
            return w.rearrange("(k p) n -> p k n", p=P)

        blocks_first = [Block(0, 0, first=True), Block(0, 1)]
        blocks_last = [Block(PAIRS - 1, 0), Block(PAIRS - 1, 1, last=True)]

        def all_pairs(eng, run):
            for blk in blocks_first:
                run(blk)
            with eng.Fori(1, PAIRS - 1) as i:
                for b in range(B):
                    run(Block(i, b))
            for blk in blocks_last:
                run(blk)

        block = ctx.enter_context(nc.Block())

        @block.sync
        def _(sp):
            for t in range(TILES):
                sp.dma_start(xn[:, t, :], x_v[0, 0, t]).then_inc(in_x[t], 16)
            sp.dma_start(ctx_raw[:], rows(ctxT)).then_inc(in_k, 16)
            sp.dma_start(wk_raw[:], rows(wkT)).then_inc(in_k, 16)
            sp.dma_start(mask_sb[:, 0], mask_v[0, 0]).then_inc(in_mask[0], 16)
            for t in range(TILES):
                sp.dma_start(res[:, t, :], x_v[0, 0, t]).then_inc(in_res[t], 16)
            for t in range(TILES):
                sp.wait_ge(job_done, t + 1)
                sp.dma_start(xn[:, t, :], x_v[1, 0, t]).then_inc(in_x[t], 16)

            def attention(blk):
                b, last_pair = blk.b, isinstance(blk.i, int) and blk.i == PAIRS - 1
                if not blk.last:
                    wait(sp, masked, blk.at(UNITS))
                    sp.dma_start(mask_sb[:, 1 - b], mask_v[1 - b, blk.i + b]).then_inc(in_mask[1 - b], 16)
                if not blk.first:
                    for t in range(TILES):
                        sp.wait_ge(job_out, blk.job("o", t) + 1)
                        sp.dma_start(x2_v[1 - b, blk.i - (1 - b), t], res[:, t, :]).then_inc(stored[t], 16)
                    for t in range(TILES):
                        sp.wait_ge(stored[t], blk.at(16))
                        sp.dma_start(res[:, t, :], x_v[b, blk.i, t]).then_inc(in_res[t], 16)
                for t in range(TILES):
                    sp.wait_ge(job_done, blk.job("x", t) + 1)
                    src = x2_n[b, t] if last_pair else x_v[b, blk.i + 1, t]
                    sp.dma_start(xn[:, t, :], src).then_inc(in_x[t], 16)

            all_pairs(sp, attention)

            def load_chunk(m):
                r = m % STAGE
                sp.dma_start(w_stage[:, r, 0, :].rearrange("p (k j) -> p k j", j=P), w1_v[m]).then_inc(in_w[r], 16)
                sp.dma_start(w_stage[:, r, 1, :], w2_v[m]).then_inc(in_w[r], 16)

            sp.wait_ge(wq_step, 2)
            sp.wait_ge(wo_step, 2)
            for m in range(STAGE):
                load_chunk(m)
            for t in range(TILES):
                sp.wait_ge(job_out, O_LAST + t + 1)
                sp.dma_start(x2_v[B - 1, PAIRS - 1, t], res[:, t, :]).then_inc(stored[t], 16)
            for m in range(STAGE, 2 * STAGE):
                sp.wait_ge(w_step, 4 * (m - STAGE + 1))
                load_chunk(m)
            for t in range(TILES):
                sp.wait_ge(stored[t], 16 * NB)
                sp.dma_start(res[:, t, :], x2_n[0, t]).then_inc(in_res[t], 16)
            for m in range(2 * STAGE, MC):
                sp.wait_ge(w_step, 4 * (m - STAGE + 1))
                load_chunk(m)

            def store_and_reload(n, reload_res, reload_x):
                if reload_x:
                    for t in range(TILES):
                        sp.wait_ge(job_done, n * TILES + (FFN_JOB + t + 1))
                        sp.dma_start(xn[:, t, :], x2_n[n + 2, t]).then_inc(in_x[t], 16)
                for t in range(TILES):
                    sp.wait_ge(summed, n * TILES + (t + 1))
                    sp.dma_start(out_n[n, t], res[:, t, :]).then_inc(stored[t], 16)
                if reload_res:
                    for t in range(TILES):
                        sp.wait_ge(stored[t], n * 16 + 16 * (NB + 1))
                        sp.dma_start(res[:, t, :], x2_n[n + 1, t]).then_inc(in_res[t], 16)

            with sp.Fori(0, NB - 2) as n:
                store_and_reload(n, True, True)
            store_and_reload(NB - 2, True, False)
            store_and_reload(NB - 1, False, False)
            for t in range(TILES):
                sp.wait_ge(stored[t], 16 * 2 * NB)

        @block.tensor
        def _(pe):
            def three(out_ap, a_hi, a_lo, b_hi, b_lo, start, stop):
                pe.matmul(out_ap, a_lo, b_hi, start=start, stop=False)
                pe.matmul(out_ap, a_hi, b_lo, start=False, stop=False)
                return pe.matmul(out_ap, a_hi, b_hi, start=False, stop=stop)

            def job_bank(job, n):
                wait(pe, job_out, job - 1)
                return JOB_BANK[n]

            def q_job(job, bank_no, c):
                dst = job_bank(job, bank_no)
                for k in range(KC):
                    w = slice(c * P, (c + 1) * P)
                    last = three(dst[:, :], wq_hi[:, k, w], wq_lo[:, k, w], xT_hi[:, k, :], xT_lo[:, k, :],
                                 k == 0, k == KC - 1)
                last.then_inc(job_done, 1)

            def x_job(job, bank_no, t, ready):
                dst = job_bank(job, bank_no)
                pe.wait_ge(normed, ready)
                for k in range(KC):
                    last = pe.transpose(dst[:, k * P:(k + 1) * P], xn[:, t, k * P:(k + 1) * P], ident[:, :])
                last.then_inc(job_done, 1)

            def o_job(job, bank_no, t):
                dst = job_bank(job, bank_no)
                for c in range(GROUPS):
                    tok = slice(t * P, (t + 1) * P)
                    last = three(dst[:, :], oT_hi[:, c, tok], oT_lo[:, c, tok], wo_hi[:, c, :], wo_lo[:, c, :],
                                 c == 0, c == GROUPS - 1)
                last.then_inc(job_done, 1)

            def scores(blk, u):
                c, t = divmod(u, TILES)
                wait(pe, masked, blk.at(UNITS, u - 1))
                if t == 0:
                    pe.wait_ge(job_out, blk.q_ready(c))
                tok = slice(t * P, (t + 1) * P)
                three(S_BANK[u % 2][:, :], qT_hi[:, c % 2, tok], qT_lo[:, c % 2, tok],
                      kbd_hi[:, blk.b, c, :], kbd_lo[:, blk.b, c, :], True, True).then_inc(scored, 1)

            def turn(blk, u):
                t = u % TILES
                pe.wait_ge(scaled, blk.at(UNITS, u + 1))
                wait(pe, pT_ready, blk.at(UNITS, u - 1))
                for j in range(4):
                    last = pe.transpose(T_BANK[u % 2][:, j * P:(j + 1) * P], pr[:, t, j, :], ident[:, :])
                last.then_inc(turned, 1)

            def p_v(blk, c):
                back = GROUPS if c == 3 else 0
                b = 1 - blk.b if c == 3 else blk.b
                group = blk.at(GROUPS, c - back)
                pe.wait_ge(pT_ready, blk.at(UNITS, UNITS // GROUPS * (c - back + 1)))
                wait(pe, oT_ready, group - 1)
                for j in range(4):
                    h = 4 * c + j
                    last = pe.matmul(PV_BANK[c % 2][j * DK:(j + 1) * DK, :], v_sb[:, b, h * DK:(h + 1) * DK],
                                     pT[:, c % 2, j, :], start=True, stop=True)
                last.then_inc(pv_done, 1)

            pe.wait_ge(made, 1)
            for t in range(TILES):
                x_job(t, t % 2, t, t + 1)
            pe.wait_ge(in_k, 32)
            for c in range(GROUPS):
                for k in range(KC):
                    last = pe.matmul(bank[c][:, 0:B * KEYS], wk_raw[:, k, c * P:(c + 1) * P], ctx_raw[:, k, :],
                                     start=(k == 0), stop=(k == KC - 1))
                last.then_inc(k_done, 1)
            pe.wait_ge(wq_step, 2)
            pe.wait_ge(job_out, TILES)
            q_job(TILES, TILES % 2, 0)
            pe.wait_ge(in_v, 16)
            for b in range(B):
                for k in range(KC):
                    last = pe.matmul(bank[4 + b][:, :], ctx_raw[:, k, b * KEYS:(b + 1) * KEYS], wv_raw[:, k, :],
                                     start=(k == 0), stop=(k == KC - 1))
                last.then_inc(v_done, 1)
            pe.wait_ge(kv_step, KV_STEPS)
            pe.wait_ge(wo_step, 2)

            def attention(blk):
                for u in range(UNITS):
                    scores(blk, u)
                    if not (blk.first and u < LAG):
                        turn(blk, u - LAG)
                    for kind, which, job, _ in blk.jobs(u):
                        n = blk.bank(kind, which)
                        if kind == "x":
                            x_job(job, n, which, blk.at(TILES, TILES + which + 1))
                        elif kind == "o":
                            if which == 0:
                                pe.wait_ge(oT_ready, blk.at(GROUPS))
                            o_job(job, n, which)
                        else:
                            if kind == "q0":
                                pe.wait_ge(job_out, blk.job("x", TILES - 1) + 1)
                            q_job(job, n, which)
                    if u in PV_SLOTS and not (blk.first and PV_SLOTS[u] == 3):
                        p_v(blk, PV_SLOTS[u])

            all_pairs(pe, attention)
            end = Block(PAIRS, 0)
            for u in range(-LAG, 0):
                turn(end, u)
            p_v(end, 3)
            pe.wait_ge(oT_ready, GROUPS * NB)
            for t in range(TILES):
                o_job(O_LAST + t, (O_LAST + t) % 2, t)

            pe.wait_ge(masked, UNITS * NB)
            pe.wait_ge(pT_ready, UNITS * NB)

            def up(n, m):
                g = n * MC + m
                wait(pe, relued, g - 1)
                pe.wait_ge(w_step, 4 * m + 2)
                for k in range(KC):
                    w = slice(k * P, (k + 1) * P)
                    last = three(UP_BANK[m % 2][:, :], w_chunk[m][:, 0, w], w_chunk[m][:, 1, w],
                                 xT_hi[:, k, :], xT_lo[:, k, :], k == 0, k == KC - 1)
                last.then_inc(up_done, 1)

            def down(n, m):
                pe.wait_ge(h_ready, n * MC + (m + 1))
                pe.wait_ge(w_step, 4 * m + 4)
                for t in range(TILES):
                    if m == 0:
                        wait(pe, summed, n * TILES + (t + 1 - TILES))
                    tok = slice(t * P, (t + 1) * P)
                    last = three(ACC_BANK[t][:, :], h_hi[:, m % 2, tok], h_lo[:, m % 2, tok],
                                 w_chunk[m][:, 2, :], w_chunk[m][:, 3, :], m == 0, m == MC - 1)
                last.then_inc(down_done, 1)

            def feed_forward(n, last_block=False):
                pe.wait_ge(job_out, n * TILES + FFN_JOB)
                up(n, 0)
                for m in range(1, MC):
                    up(n, m)
                    if m < MC - 1:
                        down(n, m - 1)
                for t in range(TILES):
                    if not last_block:
                        x_job(n * TILES + (FFN_JOB + t), (FFN_JOB + t) % 2, t, n * TILES + (TILES * (NB + 1) + t + 1))
                    if t == 1:
                        down(n, MC - 2)
                down(n, MC - 1)

            feed_forward(0)
            with pe.Fori(1, NB - 1) as n:
                feed_forward(n)
            feed_forward(NB - 1, last_block=True)

        @block.scalar
        def _(act):
            act.dma_start(bk_col[:], bk).then_inc(in_cols, 16)
            act.dma_start(bq_col[:], bq).then_inc(in_cols, 16)
            act.dma_start(b1_col[:], b1).then_inc(in_cols, 16)
            act.dma_start(wq_raw[:], rows(wqT)).then_inc(in_wq, 16)
            act.dma_start(wv_raw[:], rows(wvT)).then_inc(in_v, 16)
            act.dma_start(bv_row[:], bv.to_broadcast([P, D])).then_inc(in_rows, 16)
            act.dma_start(bo_row[:], bo.to_broadcast([P, D])).then_inc(in_rows, 16)
            act.dma_start(wo_raw[:], rows(woT)).then_inc(in_wo, 16)
            act.dma_start(b2_row[:], b2.to_broadcast([P, D])).then_inc(in_rows, 16)

            def x_hi(job, n, t):
                act.wait_ge(job_done, job + 1)
                act.activation(xT_hi[:, :, t * P:(t + 1) * P], JOB_BANK[n][:, :].rearrange("p (k j) -> p k j", j=P),
                               ACT.Copy).then_inc(job_hi, 1)

            def q_hi(job, n, c, units):
                act.wait_ge(job_done, job + 1)
                wait(act, scored, units)
                act.activation(qT_hi[:, c % 2, :], JOB_BANK[n][:, :], ACT.Identity,
                               bias=bq_col[:, c:c + 1]).then_inc(job_hi, 1)

            def pT_out(blk, u):
                c, t = divmod(u % UNITS, TILES)
                act.wait_ge(turned, blk.at(UNITS, u + 1))
                if t == 0:
                    wait(act, pv_done, blk.at(GROUPS, u // TILES - 1))
                act.activation(pT[:, c % 2, :, t * P:(t + 1) * P],
                               T_BANK[u % 2][:, :].rearrange("p (h j) -> p h j", j=P), ACT.Copy).then_inc(pT_ready, 1)

            def exps(blk, u):
                t = u % TILES
                act.wait_ge(maxed, blk.at(UNITS, u + 1))
                wait(act, turned, blk.at(UNITS, u - 3))
                for j in range(4):
                    last = act.activation(pr[:, t, j, :], sc[:, t, j, :], ACT.Exp, bias=neg_max[:, t, j:j + 1],
                                          accum_out=row_sum[:, t, j:j + 1])
                last.then_inc(exped, 1)

            def oT_out(blk, c):
                back = GROUPS if c == 3 else 0
                act.wait_ge(pv_done, blk.at(GROUPS, c - back + 1))
                act.activation(oT_hi[:, c, :], PV_BANK[c % 2][:, :], ACT.Copy).then_inc(oT_hi_done, 1)

            for t in range(TILES):
                x_hi(t, t % 2, t)
            act.wait_ge(in_cols, 48)
            q_hi(TILES, TILES % 2, 0, 0)
            act.wait_ge(kv_step, KV_STEPS)

            def attention(blk):
                for u in range(UNITS):
                    if not (blk.first and u < LAG):
                        pT_out(blk, u - LAG)
                    exps(blk, u)
                    for kind, which, job, _ in blk.jobs(u):
                        n = blk.bank(kind, which)
                        if kind == "x":
                            x_hi(job, n, which)
                        elif kind == "q":
                            q_hi(job, n, which, blk.at(UNITS, TILES * (which - 1)))
                        elif kind == "q0":
                            q_hi(job, n, 0, blk.at(UNITS, TILES * (GROUPS - 1)))
                    if u in PV_SLOTS and not (blk.first and PV_SLOTS[u] == 3):
                        oT_out(blk, PV_SLOTS[u])

            all_pairs(act, attention)
            end = Block(PAIRS, 0)
            for u in range(-LAG, 0):
                pT_out(end, u)
            oT_out(end, 3)

            def feed_forward(n, last_block=False):
                for m in range(MC):
                    g = n * MC + m
                    act.wait_ge(up_done, g + 1)
                    wait(act, h_ready, g - 1)
                    act.activation(h_raw[:, m % 2, :], UP_BANK[m % 2][:, :], ACT.Relu,
                                   bias=b1_col[:, m:m + 1]).then_inc(relued, 1)
                if not last_block:
                    for t in range(TILES):
                        x_hi(n * TILES + (FFN_JOB + t), (FFN_JOB + t) % 2, t)

            feed_forward(0)
            with act.Fori(1, NB - 1) as n:
                feed_forward(n)
            feed_forward(NB - 1, last_block=True)

        @block.vector
        def _(dve):
            def count(k_x, t, ready):
                dve.wait_ge(in_x[t], ready)
                dve.bn_stats(stats[:, t, :], xn[:, t, :]).then_inc(counted, 1)

            def mean(done, t):
                dve.wait_ge(counted, done + 1)
                wait(dve, normed, done - t)
                dve.sem_inc(passed, 1)
                dve.bn_aggr(mean_var[:, t, :], stats[:, t, :]).then_inc(meaned, 1)

            def normalise(t, ready):
                dve.wait_ge(rstd_ready, ready)
                dve.tensor_scalar(xn[:, t, :], xn[:, t, :], mean_var[:, t, 0:1], rstd[:, t:t + 1],
                                  ALU.subtract, ALU.mult).then_inc(normed, 1)

            def x_lo(hi_no, n, t):
                dve.wait_ge(job_hi, hi_no + 1)
                tok = slice(t * P, (t + 1) * P)
                dve.tensor_tensor(xT_lo[:, :, tok], JOB_BANK[n][:, :].rearrange("p (k j) -> p k j", j=P),
                                  xT_hi[:, :, tok].bitcast(F32), ALU.subtract).then_inc(job_out, 1)

            def q_lo(hi_no, n, c):
                dve.wait_ge(job_hi, hi_no + 1)
                dve.scalar_tensor_tensor(out=qT_lo[:, c % 2, :], in0=JOB_BANK[n][:, :], scalar=bq_col[:, c:c + 1],
                                         in1=qT_hi[:, c % 2, :].bitcast(F32), op0=ALU.add,
                                         op1=ALU.subtract).then_inc(job_out, 1)

            def x2_sum(job, n, t, ready):
                dve.wait_ge(job_done, job + 1)
                dve.wait_ge(biased, ready)
                dve.tensor_tensor(res[:, t, :], JOB_BANK[n][:, :], res[:, t, :], ALU.add).then_inc(job_out, 1)

            def oT_low(blk, c):
                back = GROUPS if c == 3 else 0
                dve.wait_ge(oT_hi_done, blk.at(GROUPS, c - back + 1))
                dve.tensor_tensor(oT_lo[:, c, :], PV_BANK[c % 2][:, :], oT_hi[:, c, :].bitcast(F32),
                                  ALU.subtract).then_inc(oT_ready, 1)

            dve.memset(kbd_lo[:].bitcast(F32), 0.0).then_inc(kv_step, 1)
            for t in range(TILES):
                count(0, t, 16)
                mean(t, t)
            for t in range(TILES):
                normalise(t, 1)
            dve.wait_ge(in_wq, 16)
            dve.tensor_copy(wq_hi[:], wq_raw[:]).then_inc(wq_step, 1)
            for t in range(TILES):
                x_lo(t, t % 2, t)
            dve.wait_ge(wq_step, 1)
            dve.tensor_tensor(wq_lo[:], wq_raw[:], wq_hi[:].bitcast(F32), ALU.subtract).then_inc(wq_step, 1)
            dve.wait_ge(in_cols, 48)
            for c in range(GROUPS):
                dve.wait_ge(k_done, c + 1)
                last = dve.tensor_scalar(k_raw[:, c], bank[c][:, 0:B * KEYS].rearrange("p (b k) -> p b k", b=B),
                                         bk_col[:, c:c + 1], float(DK) ** -0.5, ALU.add, ALU.mult)
                last.then_inc(kv_step, 1)
            dve.wait_ge(kv_step, 1 + GROUPS)
            dve.wait_ge(made, 2)

            def head(t, j):
                return t[j * DK:(j + 1) * DK, :, :, j * KEYS:(j + 1) * KEYS]

            def k_head(j):
                return k_raw[j * DK:(j + 1) * DK].rearrange("p c b k -> p b c k")

            for j in range(4):
                dve.tensor_copy(head(kbd_hi, j), k_head(j)).then_inc(kv_step, 1)
            q_lo(TILES, TILES % 2, 0)
            for j in range(4):
                dve.wait_ge(kv_step, 1 + GROUPS + j + 1)
                dve.tensor_tensor(head(kbd_lo, j), k_head(j), head(kbd_hi, j).bitcast(F32),
                                  ALU.subtract).then_inc(kv_step, 1)
            dve.wait_ge(in_rows, 48)
            for b in range(B):
                dve.wait_ge(v_done, b + 1)
                dve.tensor_tensor(v_sb[:, b, :], bank[4 + b][:, :], bv_row[:], ALU.add).then_inc(kv_step, 1)

            def late(blk, u):
                for kind, which, job, hi_no in blk.jobs(u):
                    n = blk.bank(kind, which)
                    if kind == "x":
                        x_lo(hi_no, n, which)
                    elif kind == "o":
                        x2_sum(job, n, which, blk.at(TILES, which + 1 - TILES))
                    else:
                        q_lo(hi_no, n, which)
                if u in PV_SLOTS and not (blk.first and PV_SLOTS[u] == 3):
                    oT_low(blk, PV_SLOTS[u])

            def invert(blk, u):
                t = u % TILES
                dve.wait_ge(exped, blk.at(UNITS, u + 1))
                wait(dve, scaled, blk.at(UNITS, u - 3))
                dve.reciprocal(row_inv[:, t, :], row_sum[:, t, :]).then_inc(inverted, 1)

            def attention(blk):
                for u in range(UNITS):
                    c, t = divmod(u, TILES)
                    dve.wait_ge(scored, blk.at(UNITS, u + 1))
                    wait(dve, exped, blk.at(UNITS, u - 3))
                    if c == 0:
                        dve.wait_ge(filled, blk.at(TILES, t + 1))
                    if u == 0:
                        dve.wait_ge(in_mask[blk.b], blk.i * 16 + 16)
                    dve.sem_inc(passed, 1)
                    dve.copy_predicated(sc[:, t], mask_sb[:, blk.b, t, :].unsqueeze(1).to_broadcast([P, 4, KEYS]),
                                        S_BANK[u % 2][:, :].rearrange("p (h k) -> p h k", k=KEYS)).then_inc(masked, 1)
                    if u in STATS_SLOTS:
                        count(None, STATS_SLOTS[u], blk.at(16, 32))
                    if not (blk.first and u == 0):
                        invert(blk, u - 1)
                    dve.wait_ge(masked, blk.at(UNITS, u + 1))
                    dve.tensor_reduce(neg_max[:, t, :], sc[:, t], AX.X, ALU.max, negate=True).then_inc(maxed, 1)
                    if u in STATS_SLOTS:
                        mean(blk.at(TILES, TILES + STATS_SLOTS[u]), STATS_SLOTS[u])
                    if u == 0 and not blk.first:
                        oT_low_prev(blk)
                    if u > 0:
                        late(blk, u - 1)
                    if u in APPLY_SLOTS:
                        normalise(APPLY_SLOTS[u], blk.at(1, 2))

            def oT_low_prev(blk):
                dve.wait_ge(oT_hi_done, blk.at(GROUPS, -1))
                dve.tensor_tensor(oT_lo[:, 2, :], PV_BANK[0][:, :], oT_hi[:, 2, :].bitcast(F32),
                                  ALU.subtract).then_inc(oT_ready, 1)

            all_pairs(dve, attention)
            end = Block(PAIRS, 0)
            invert(end, -1)
            oT_low_prev(end)
            oT_low(end, 3)
            for t in range(TILES):
                x2_sum(O_LAST + t, (O_LAST + t) % 2, t, TILES * (NB - 1) + t + 1)

            def feed_forward(n, last_block=False):
                for m in range(MC):
                    g = n * MC + m
                    dve.wait_ge(relued, g + 1)
                    wait(dve, down_done, g - 1)
                    dve.tensor_copy(h_hi[:, m % 2, :], h_raw[:, m % 2, :]).then_inc(hi_done, 1)
                    if 2 <= m < 2 + TILES and not last_block:
                        count(None, m - 2, n * 16 + 16 * (NB + 2))
                    dve.wait_ge(hi_done, g + 1)
                    dve.tensor_tensor(h_lo[:, m % 2, :], h_raw[:, m % 2, :], h_hi[:, m % 2, :].bitcast(F32),
                                      ALU.subtract).then_inc(h_ready, 1)
                    if 2 <= m < 2 + TILES and not last_block:
                        mean(n * TILES + (TILES * (NB + 1) + m - 2), m - 2)
                    if MC - 1 - TILES <= m < MC - 1 and not last_block:
                        normalise(m - (MC - 1 - TILES), n + (NB + 2))
                if not last_block:
                    for t in range(TILES):
                        x_lo(n * TILES + (FFN_HI + t), (FFN_JOB + t) % 2, t)
                for t in range(TILES):
                    dve.wait_ge(down_done, n * MC + MC)
                    dve.wait_ge(biased, n * TILES + (TILES * NB + t + 1))
                    dve.tensor_tensor(res[:, t, :], ACC_BANK[t][:, :], res[:, t, :], ALU.add).then_inc(summed, 1)

            feed_forward(0)
            with dve.Fori(1, NB - 1) as n:
                feed_forward(n)
            feed_forward(NB - 1, last_block=True)

        @block.gpsimd
        def _(pool):
            def split(raw, hi, lo, sem_, before):
                pool.tensor_scalar(hi, raw, 1.0, 0.0, ALU.mult, ALU.add).then_inc(sem_, 1)
                pool.wait_ge(sem_, before + 1)
                pool.tensor_tensor(lo, raw, hi.bitcast(F32), ALU.subtract).then_inc(sem_, 1)

            def rstds(ready):
                pool.wait_ge(meaned, ready * TILES)
                pool.tensor_tensor(rstd[:], mean_var[:, :, 1], eps[:], ALU.add).then_inc(eps_added, 1)
                pool.wait_ge(eps_added, ready)
                pool.tensor_tensor(rstd[:], rstd[:], minus_half[:], ALU.pow).then_inc(rstd_ready, 1)

            def add_bias(t, landed, row):
                pool.wait_ge(in_res[t], landed)
                pool.tensor_tensor(res[:, t, :], res[:, t, :], row[:], ALU.add).then_inc(biased, 1)

            def fill(t):
                pool.memset(sc[:, t], MASKED).then_inc(filled, 1)

            def scale(blk, u):
                t = u % TILES
                pool.wait_ge(inverted, blk.at(UNITS, u + 1))
                pool.tensor_tensor(pr[:, t], pr[:, t], row_inv[:, t, :].unsqueeze(2).to_broadcast([P, 4, KEYS]),
                                   ALU.mult).then_inc(scaled, 1)

            pool.memset(minus_half[:], -0.5).then_inc(zeroed, 1)
            pool.memset(eps[:], EPS).then_inc(zeroed, 1)
            pool.memset(ident[:], 0.0).then_inc(zeroed, 1)
            pool.wait_ge(zeroed, 3)
            pool.affine_select(out=ident[:], in_=ident[:], compare_op=ALU.not_equal, fill=1.0, base=0,
                               pattern=[[-1, P]], channel_multiplier=1).then_inc(made, 1)
            pool.memset(kbd_hi[:].bitcast(F32), 0.0).then_inc(made, 1)
            rstds(1)
            for t in range(TILES):
                fill(t)
            pool.wait_ge(in_wo, 16)
            split(wo_raw[:], wo_hi[:], wo_lo[:], wo_step, 0)
            pool.wait_ge(in_rows, 48)

            def attention(blk):
                for u in range(UNITS):
                    if not (blk.first and u == 0):
                        scale(blk, u - 1)
                    if u > UNITS - TILES and not blk.last:
                        fill(u - 1 - (UNITS - TILES))
                    if u == 0 and not blk.first:
                        fill(TILES - 1)
                    if u == RSTD_SLOT:
                        rstds(blk.at(1, 2))
                    if u in RESIDUAL_SLOTS:
                        add_bias(RESIDUAL_SLOTS[u], blk.at(16, 16), bo_row)

            all_pairs(pool, attention)
            scale(Block(PAIRS, 0), -1)

            for m in range(MC):
                if m == 0:
                    pool.wait_ge(scored, UNITS * NB)
                if m == early_chunks:
                    pool.wait_ge(job_done, FFN_JOB)
                pool.wait_ge(in_w[m % STAGE], 32 * (m // STAGE + 1))
                for part in range(2):
                    split(w_stage[:, m % STAGE, part, :], w_chunk[m][:, 2 * part, :], w_chunk[m][:, 2 * part + 1, :],
                          w_step, 4 * m + 2 * part)

            def feed_forward(n, last_block=False):
                for t in range(TILES):
                    add_bias(t, n * 16 + 16 * (NB + 1), b2_row)
                if not last_block:
                    rstds(n + (NB + 2))

            feed_forward(0)
            with pool.Fori(1, NB - 1) as n:
                feed_forward(n)
            feed_forward(NB - 1, last_block=True)


def kernel(x, ctx_1024, mask_Bx1xSxS2_ik0, L0_xattn_Wq, L0_xattn_bq, L0_xattn_Wk, L0_xattn_bk, L0_xattn_Wv,
           L0_xattn_bv, L0_xattn_Wo, L0_xattn_bo, L0_ffn_W1, L0_ffn_b1, L0_ffn_W2, L0_ffn_b2):
    import numpy as np
    import concourse.bacc as bacc
    from concourse.bass_utils import run_bass_kernel_spmd

    lay = np.ascontiguousarray
    x, ctx, mask = np.asarray(x), np.asarray(ctx_1024), np.asarray(mask_Bx1xSxS2_ik0)
    arrays = {
        "x": lay(x.reshape(B * S, D)),
        "ctxT": lay(ctx.reshape(B * KEYS, D).T),
        "mask": lay(mask.reshape(B * S, KEYS)),
        "wqT": lay(np.asarray(L0_xattn_Wq).T), "bq": lay(np.asarray(L0_xattn_bq).reshape(KC, P).T),
        "wkT": lay(np.asarray(L0_xattn_Wk).T), "bk": lay(np.asarray(L0_xattn_bk).reshape(KC, P).T),
        "wvT": lay(np.asarray(L0_xattn_Wv).T), "bv": lay(np.asarray(L0_xattn_bv).reshape(1, D)),
        "woT": lay(np.asarray(L0_xattn_Wo).T), "bo": lay(np.asarray(L0_xattn_bo).reshape(1, D)),
        "w1": lay(np.asarray(L0_ffn_W1)), "b1": lay(np.asarray(L0_ffn_b1).reshape(MC, P).T),
        "w2": lay(np.asarray(L0_ffn_W2)), "b2": lay(np.asarray(L0_ffn_b2).reshape(1, D)),
    }
    nc = bacc.Bacc("TRN2", target_bir_lowering=False, num_devices=1)
    args = [nc.dram_tensor(f"in_{name}", a.shape, mybir.dt.from_np(a.dtype), kind="ExternalInput").ap()
            for name, a in arrays.items()]
    x2 = nc.dram_tensor("x2_between", (B * S, D), F32, kind="Internal").ap()
    out = nc.dram_tensor("out_0", (B * S, D), F32, kind="ExternalOutput").ap()
    build(nc, *args, x2, out)
    r = run_bass_kernel_spmd(nc, [{f"in_{name}": a for name, a in arrays.items()}], core_ids=[0])
    return r.results[0]["out_0"].reshape(B, S, D)
```

```python
from contextlib import ExitStack

import concourse.bass as bass
from concourse import mybir

F32 = mybir.dt.float32
F32R = mybir.dt.float32r
I32 = mybir.dt.int32
ALU = mybir.AluOpType
ACT = mybir.ActivationFunctionType
AX = mybir.AxisListType

P = 128
B = 2
S = 2048
D = 512
KEYS = 128
H = 16
DK = D // H
INTER = 2048
BLOCK = 512
TILES = BLOCK // P
NB = B * S // BLOCK
PAIRS = NB // B
KC = D // P
GROUPS = H // 4
UNITS = GROUPS * TILES
MC = INTER // P
LAG = 3
STAGE = 3
EPS = 1e-5
MASKED = -1000000000.0

STEPS = {
    0: [("q", 1, 0, 2)], 1: [("q", 1, 2, 4)], 2: [("q", 2, 0, 2)], 3: [("q", 2, 2, 3)], 4: [("q", 2, 3, 4)],
    5: [("o", 0, 0, 3)], 6: [("o", 0, 3, 4), ("o", 1, 0, 2)], 7: [("o", 1, 2, 4)],
    8: [("q", 3, 0, 3)], 9: [("q", 3, 3, 4), ("x", 0, 0, 4), ("x", 1, 0, 4)], 10: [],
    11: [("x", 2, 0, 4), ("x", 3, 0, 4), ("o", 2, 0, 1)], 12: [("o", 2, 1, 4)],
    13: [("q0", 0, 0, 3)], 14: [("q0", 0, 3, 4), ("o", 3, 0, 2)], 15: [("o", 3, 2, 4)],
}
JOBS = [(slot, kind, which) for slot in range(UNITS) for kind, which, _, end in STEPS[slot] if end == KC]
PV_SLOTS = {3: 3, 7: 0, 11: 1, 15: 2}
STATS_SLOTS = {0: 0, 1: 1, 2: 2, 3: 3}
RSTD_SLOT = 5
APPLY_SLOTS = {6: 0, 7: 1, 8: 2, 9: 3}
BIAS_SLOTS = {1: 0, 2: 1, 6: 2, 7: 3}
V_SLOTS = {0: 0, 2: 1}
KV_STEPS = 1 + GROUPS + 4 + 4
N_PRO = TILES + 1


class Block:

    def __init__(self, i, b, first=False, last=False):
        self.i, self.b, self.first, self.last = i, b, first, last
        self.batch = b % B

    def prev(self):
        return Block(self.i, self.b - 1, first=isinstance(self.i, int) and 2 * self.i + self.b == 1)

    def unit(self, u):
        return (self, u) if u >= 0 else (self.prev(), u + UNITS)

    def at(self, per, k=0):
        return self.i * (2 * per) + (self.b * per + k)

    def has(self, kind):
        return not (kind == "o" and self.first) and not (kind == "q0" and self.last)

    def jobs(self, slot=None):
        out, j, h = [], 0, 0
        for s, kind, which in JOBS:
            if self.has(kind):
                if slot is None or s == slot:
                    job = N_PRO + j if self.first else self.at(len(JOBS), N_PRO - TILES + j)
                    out.append((kind, which, job, self.at(len(JOBS) - TILES, N_PRO + h),
                                (N_PRO + j - (0 if self.first else TILES)) % 3))
                j += 1
                h += kind != "o"
        return out

    def job(self, kind, which=0):
        return next(x[2] for x in self.jobs() if x[:2] == (kind, which))

    def bank(self, kind, which=0):
        return next(x[4] for x in self.jobs() if x[:2] == (kind, which))

    def q_ready(self, c):
        if c:
            return self.job("q", c) + 1
        return N_PRO if self.first else self.prev().job("q0") + 1

    def pv(self, slot):
        c = PV_SLOTS.get(slot)
        if c is None or (c == 3 and self.first):
            return None
        return (self.prev(), c) if c == 3 else (self, c)


O_LAST = N_PRO + len(JOBS) * NB - TILES - 1
FFN_JOB = O_LAST + TILES
FFN_HI = N_PRO + (len(JOBS) - TILES) * NB - 1


def wait(eng, sem, value):
    if not isinstance(value, int) or value > 0:
        eng.wait_ge(sem, value)


def build(nc, x, ctxT, mask, wqT, bq, wkT, bk, wvT, bv, woT, bo, w1, b1, w2, b2, x2_dram, out):
    ctx = ExitStack()
    with ctx:
        base = -(-nc.sbuf_base // 64) * 64
        top = [base]

        def sb(name, shape, dt=F32, at=None):
            size = 4
            for n in shape[1:]:
                size *= n
            where = top[0] if at is None else at
            if at is None:
                top[0] += -(-size // 64) * 64
            t = nc.alloc_sbuf_tensor_at(name, shape, dt, offset=where)
            return t

        ident = sb("ident", [P, P])
        minus_half = sb("minus_half", [P, TILES])
        eps = sb("eps", [P, TILES])
        bo_row = sb("bo_row", [P, D])
        b2_row = sb("b2_row", [P, D])
        bq_col = sb("bq_col", [P, KC])
        bk_col = sb("bk_col", [P, KC])
        b1_col = sb("b1_col", [P, MC])
        stats = sb("stats", [P, TILES, 6])
        mean_var = sb("mean_var", [P, TILES, 2])
        rstd = sb("rstd", [P, TILES])
        neg_max = sb("neg_max", [P, TILES, 4])
        row_sum = sb("row_sum", [P, TILES, 4])
        row_inv = sb("row_inv", [P, TILES, 4])
        xn = sb("xn", [P, TILES, D])
        res = sb("res", [P, TILES, D])
        xT_hi = sb("xT_hi", [P, KC, BLOCK], F32R)
        xT_lo = sb("xT_lo", [P, KC, BLOCK], F32R)
        stage_at = top[0]
        h_raw = sb("h_raw", [P, 2, BLOCK])
        h_hi = sb("h_hi", [P, 2, BLOCK], F32R)
        h_lo = sb("h_lo", [P, 2, BLOCK], F32R)
        w_stage = sb("w_stage", [P, STAGE, 2, D])
        ffn_at = top[0]
        kbd_hi = sb("kbd_hi", [P, B, GROUPS, 4 * KEYS], F32R)
        kbd_lo = sb("kbd_lo", [P, B, GROUPS, 4 * KEYS], F32R)
        wq_hi = sb("wq_hi", [P, KC, D], F32R)
        wq_lo = sb("wq_lo", [P, KC, D], F32R)
        qT_hi = sb("qT_hi", [P, 2, BLOCK], F32R)
        qT_lo = sb("qT_lo", [P, 2, BLOCK], F32R)
        early_free = top[0]
        wo_hi = sb("wo_hi", [P, KC, D], F32R)
        wo_lo = sb("wo_lo", [P, KC, D], F32R)
        v_sb = sb("v_sb", [P, B, D])
        oT_at = top[0]
        oT_hi = sb("oT_hi", [P, 2, GROUPS, BLOCK], F32R)
        oT_lo = sb("oT_lo", [P, 2, GROUPS, BLOCK], F32R)
        sc = sb("sc", [P, TILES, 4, KEYS])
        pr = sb("pr", [P, TILES, 4, KEYS])
        pT_at = top[0]
        pT = sb("pT", [P, 2, 4, BLOCK])
        mask_sb = sb("mask_sb", [P, 2, TILES, KEYS], I32)
        end_a = top[0]
        chunk_bytes = 4 * D * 4
        early_chunks = (early_free - ffn_at) // chunk_bytes
        w_chunk = [sb(f"w_chunk{m}", [P, 4, D], F32R, at=ffn_at + m * chunk_bytes) for m in range(MC)]
        assert max(end_a, ffn_at + MC * chunk_bytes) <= nc.sbuf_usable_end
        wq_raw = sb("wq_raw", [P, KC, D], at=stage_at)
        wo_raw = sb("wo_raw", [P, KC, D], at=stage_at + 4 * KC * D)
        wk_raw = sb("wk_raw", [P, KC, D], at=pT_at)
        wv_raw = sb("wv_raw", [P, KC, D], at=pT_at + 4 * KC * D)
        ctx_raw = sb("ctx_raw", [P, KC, B * KEYS], at=oT_at)
        k_raw = sb("k_raw", [P, GROUPS, B, KEYS], at=oT_at + 4 * KC * B * KEYS)
        bv_row = sb("bv_row", [P, D], at=oT_at + 8 * KC * B * KEYS)

        bank = [ctx.enter_context(nc.psum_tensor(f"bank{n}", [P, 512], F32)) for n in range(8)]
        S_BANK, T_BANK, PV_BANK, JOB_BANK = bank[0:2], bank[2:4], bank[4], bank[5:8]
        UP_BANK, ACC_BANK, TURN_BANK = bank[0:2], bank[2:6], bank[6:8]

        def sem(name):
            return ctx.enter_context(nc.semaphore(name))

        in_x = [sem(f"in_x{t}") for t in range(TILES)]
        in_res = [sem(f"in_res{t}") for t in range(TILES)]
        stored = [sem(f"stored{t}") for t in range(TILES)]
        in_mask = [sem(f"in_mask{b}") for b in range(B)]
        in_k, in_v, in_wq, in_wo = sem("in_k"), sem("in_v"), sem("in_wq"), sem("in_wo")
        in_rows, in_cols = sem("in_rows"), sem("in_cols")
        in_w = [sem(f"in_w{r}") for r in range(STAGE)]
        k_done, v_done = sem("k_done"), sem("v_done")
        scored = sem("scored")
        turned = sem("turned")
        pv_done = sem("pv_done")
        job_done = sem("job_done")
        up_done = sem("up_done")
        down_done = sem("down_done")
        exped = sem("exped")
        pT_ready = sem("pT_ready")
        job_hi = sem("job_hi")
        oT_hi_done = sem("oT_hi_done")
        relued = sem("relued")
        kv_step = sem("kv_step")
        v_ready = sem("v_ready")
        wq_step = sem("wq_step")
        masked = sem("masked")
        maxed = sem("maxed")
        inverted = sem("inverted")
        job_out = sem("job_out")
        oT_ready = sem("oT_ready")
        counted = sem("counted")
        meaned = sem("meaned")
        normed = sem("normed")
        hi_done = sem("hi_done")
        h_ready = sem("h_ready")
        summed = sem("summed")
        passed = sem("passed")
        zeroed = sem("zeroed")
        made = sem("made")
        filled = sem("filled")
        scaled = sem("scaled")
        eps_added = sem("eps_added")
        rstd_ready = sem("rstd_ready")
        biased = sem("biased")
        wo_step = sem("wo_step")
        w_step = sem("w_step")

        x_v = x.rearrange("(b i t p) d -> b i t p d", b=B, i=PAIRS, t=TILES)
        mask_v = mask.rearrange("(b i t p) k -> b i p t k", b=B, i=PAIRS, t=TILES)
        x2_v = x2_dram.rearrange("(b i t p) d -> b i t p d", b=B, i=PAIRS, t=TILES)
        x2_n = x2_dram.rearrange("(n t p) d -> n t p d", n=NB, t=TILES)
        out_n = out.rearrange("(n t p) d -> n t p d", n=NB, t=TILES)
        w1_v = w1.rearrange("(k p) (m j) -> m p k j", p=P, j=P)
        w2_v = w2.rearrange("(m p) d -> m p d", p=P)

        def rows(w):
            return w.rearrange("(k p) n -> p k n", p=P)

        blocks_first = [Block(0, 0, first=True), Block(0, 1)]
        blocks_last = [Block(PAIRS - 1, 0), Block(PAIRS - 1, 1, last=True)]

        def all_pairs(eng, run):
            for blk in blocks_first:
                run(blk)
            with eng.Fori(1, PAIRS - 1) as i:
                for b in range(B):
                    run(Block(i, b))
            for blk in blocks_last:
                run(blk)

        block = ctx.enter_context(nc.Block())

        @block.sync
        def _(sp):
            for t in range(TILES):
                sp.dma_start(xn[:, t, :], x_v[0, 0, t]).then_inc(in_x[t], 16)
            sp.dma_start(ctx_raw[:], rows(ctxT)).then_inc(in_k, 16)
            sp.dma_start(wk_raw[:], rows(wkT)).then_inc(in_k, 16)
            sp.dma_start(mask_sb[:, 0], mask_v[0, 0]).then_inc(in_mask[0], 16)
            for t in range(TILES):
                sp.dma_start(res[:, t, :], x_v[0, 0, t]).then_inc(in_res[t], 16)
            for t in range(TILES):
                sp.wait_ge(job_done, t + 1)
                sp.dma_start(xn[:, t, :], x_v[1, 0, t]).then_inc(in_x[t], 16)

            def attention(blk):
                b, last_pair = blk.b, isinstance(blk.i, int) and blk.i == PAIRS - 1

                def store(t):
                    sp.wait_ge(job_out, blk.job("o", t) + 1)
                    sp.dma_start(x2_v[1 - b, blk.i - (1 - b), t], res[:, t, :]).then_inc(stored[t], 16)

                def residual(t):
                    sp.wait_ge(stored[t], blk.at(16))
                    sp.dma_start(res[:, t, :], x_v[b, blk.i, t]).then_inc(in_res[t], 16)

                if not blk.last:
                    wait(sp, masked, blk.at(UNITS))
                    sp.dma_start(mask_sb[:, 1 - b], mask_v[1 - b, blk.i + b]).then_inc(in_mask[1 - b], 16)
                if not blk.first:
                    store(0)
                    store(1)
                for t in range(TILES):
                    sp.wait_ge(job_done, blk.job("x", t) + 1)
                    src = x2_n[b, t] if last_pair else x_v[b, blk.i + 1, t]
                    sp.dma_start(xn[:, t, :], src).then_inc(in_x[t], 16)
                if not blk.first:
                    residual(0)
                    residual(1)
                    store(2)
                    store(3)
                    residual(2)
                    residual(3)

            all_pairs(sp, attention)

            def load_chunk(m):
                r = m % STAGE
                sp.dma_start(w_stage[:, r, 0, :].rearrange("p (k j) -> p k j", j=P), w1_v[m]).then_inc(in_w[r], 16)
                sp.dma_start(w_stage[:, r, 1, :], w2_v[m]).then_inc(in_w[r], 16)

            sp.wait_ge(wq_step, 2)
            sp.wait_ge(wo_step, 2)
            for m in range(STAGE):
                load_chunk(m)
            for t in range(TILES):
                sp.wait_ge(job_out, O_LAST + t + 1)
                sp.dma_start(x2_v[B - 1, PAIRS - 1, t], res[:, t, :]).then_inc(stored[t], 16)
            for m in range(STAGE, 2 * STAGE):
                sp.wait_ge(w_step, 4 * (m - STAGE + 1))
                load_chunk(m)
            for t in range(TILES):
                sp.wait_ge(stored[t], 16 * NB)
                sp.dma_start(res[:, t, :], x2_n[0, t]).then_inc(in_res[t], 16)
            for m in range(2 * STAGE, MC):
                sp.wait_ge(w_step, 4 * (m - STAGE + 1))
                load_chunk(m)

            def store_and_reload(n, reload_res, reload_x):
                if reload_x:
                    for t in range(TILES):
                        sp.wait_ge(job_done, n * TILES + (FFN_JOB + t + 1))
                        sp.dma_start(xn[:, t, :], x2_n[n + 2, t]).then_inc(in_x[t], 16)
                for t in range(TILES):
                    sp.wait_ge(summed, n * TILES + (t + 1))
                    sp.dma_start(out_n[n, t], res[:, t, :]).then_inc(stored[t], 16)
                if reload_res:
                    for t in range(TILES):
                        sp.wait_ge(stored[t], n * 16 + 16 * (NB + 1))
                        sp.dma_start(res[:, t, :], x2_n[n + 1, t]).then_inc(in_res[t], 16)

            with sp.Fori(0, NB - 2) as n:
                store_and_reload(n, True, True)
            store_and_reload(NB - 2, True, False)
            store_and_reload(NB - 1, False, False)
            for t in range(TILES):
                sp.wait_ge(stored[t], 16 * 2 * NB)

        @block.tensor
        def _(pe):
            def three(out_ap, a_hi, a_lo, b_hi, b_lo, start, stop):
                pe.matmul(out_ap, a_lo, b_hi, start=start, stop=False)
                pe.matmul(out_ap, a_hi, b_lo, start=False, stop=False)
                return pe.matmul(out_ap, a_hi, b_hi, start=False, stop=stop)

            def job_steps(job, dst, free, kind, which, k0, k1, blk=None, ready=None):
                if k0 == 0:
                    wait(pe, job_out, free)
                    if kind == "x":
                        pe.wait_ge(normed, ready)
                tok = slice(which * P, (which + 1) * P)
                for k in range(k0, k1):
                    w = slice(k * P, (k + 1) * P)
                    if kind == "x":
                        last = pe.transpose(dst[:, w], xn[:, which, w], ident[:, :])
                    elif kind == "o":
                        par = 1 - blk.batch
                        last = three(dst[:, :], oT_hi[:, par, k, tok], oT_lo[:, par, k, tok], wo_hi[:, k, :],
                                     wo_lo[:, k, :], k == 0, k == KC - 1)
                    else:
                        last = three(dst[:, :], wq_hi[:, k, tok], wq_lo[:, k, tok], xT_hi[:, k, :], xT_lo[:, k, :],
                                     k == 0, k == KC - 1)
                if k1 == KC:
                    last.then_inc(job_done, 1)

            def scores(blk, u):
                c, t = divmod(u, TILES)
                wait(pe, masked, blk.at(UNITS, u - 1))
                if t == 0:
                    pe.wait_ge(job_out, blk.q_ready(c))
                tok = slice(t * P, (t + 1) * P)
                three(S_BANK[u % 2][:, :], qT_hi[:, c % 2, tok], qT_lo[:, c % 2, tok],
                      kbd_hi[:, blk.batch, c, :], kbd_lo[:, blk.batch, c, :], True, True).then_inc(scored, 1)

            def turn(blk, u):
                t = u % TILES
                pe.wait_ge(scaled, blk.at(UNITS, u + 1))
                wait(pe, pT_ready, blk.at(UNITS, u - 1))
                for j in range(4):
                    last = pe.transpose(T_BANK[u % 2][:, j * P:(j + 1) * P], pr[:, t, j, :], ident[:, :])
                last.then_inc(turned, 1)

            def p_v(blk, c):
                if blk.first and c == 0:
                    pe.wait_ge(v_ready, B)
                pe.wait_ge(pT_ready, blk.at(UNITS, TILES * (c + 1)))
                wait(pe, oT_ready, blk.at(GROUPS, c))
                for j in range(4):
                    h = 4 * c + j
                    last = pe.matmul(PV_BANK[j * DK:(j + 1) * DK, :], v_sb[:, blk.batch, h * DK:(h + 1) * DK],
                                     pT[:, c % 2, j, :], start=True, stop=True)
                last.then_inc(pv_done, 1)

            def v_product(b):
                wait(pe, v_ready, b)
                for k in range(KC):
                    last = pe.matmul(PV_BANK[:, :], ctx_raw[:, k, b * KEYS:(b + 1) * KEYS], wv_raw[:, k, :],
                                     start=(k == 0), stop=(k == KC - 1))
                last.then_inc(v_done, 1)

            pe.wait_ge(made, 1)
            for t in range(TILES):
                job_steps(t, JOB_BANK[t % 3], t - 2, "x", t, 0, KC, ready=t + 1)
            pe.wait_ge(in_k, 32)
            for c in range(GROUPS):
                for k in range(KC):
                    last = pe.matmul(bank[c][:, 0:B * KEYS], wk_raw[:, k, c * P:(c + 1) * P], ctx_raw[:, k, :],
                                     start=(k == 0), stop=(k == KC - 1))
                last.then_inc(k_done, 1)
            pe.wait_ge(wq_step, 2)
            pe.wait_ge(job_out, TILES)
            job_steps(TILES, JOB_BANK[TILES % 3], TILES - 2, "q0", 0, 0, KC)
            pe.wait_ge(kv_step, KV_STEPS)

            def attention(blk):
                for u in range(UNITS):
                    scores(blk, u)
                    if not (blk.first and u < LAG):
                        turn(*blk.unit(u - LAG))
                    for kind, which, k0, k1 in STEPS[u]:
                        if not blk.has(kind):
                            continue
                        if k0 == 0 and kind == "o" and which == 0:
                            pe.wait_ge(oT_ready, blk.at(GROUPS))
                            if blk.b == 1 and blk.prev().first:
                                pe.wait_ge(wo_step, 2)
                        if k0 == 0 and kind == "q0":
                            pe.wait_ge(job_out, blk.job("x", TILES - 1) + 1)
                        job = blk.job(kind, which)
                        job_steps(job, JOB_BANK[blk.bank(kind, which)], job - 2, kind, which, k0, k1, blk,
                                  blk.at(TILES, TILES + which + 1))
                    if blk.first and u in V_SLOTS:
                        if u == min(V_SLOTS):
                            pe.wait_ge(in_v, 16)
                        v_product(V_SLOTS[u])
                    if blk.pv(u):
                        p_v(*blk.pv(u))

            all_pairs(pe, attention)

            def up(n, m):
                g = n * MC + m
                wait(pe, relued, g - 1)
                pe.wait_ge(w_step, 4 * m + 2)
                for k in range(KC):
                    w = slice(k * P, (k + 1) * P)
                    last = three(UP_BANK[m % 2][:, :], w_chunk[m][:, 0, w], w_chunk[m][:, 1, w],
                                 xT_hi[:, k, :], xT_lo[:, k, :], k == 0, k == KC - 1)
                last.then_inc(up_done, 1)

            def down(n, m):
                pe.wait_ge(h_ready, n * MC + (m + 1))
                pe.wait_ge(w_step, 4 * m + 4)
                for t in range(TILES):
                    if m == 0:
                        wait(pe, summed, n * TILES + (t + 1 - TILES))
                    tok = slice(t * P, (t + 1) * P)
                    last = three(ACC_BANK[t][:, :], h_hi[:, m % 2, tok], h_lo[:, m % 2, tok],
                                 w_chunk[m][:, 2, :], w_chunk[m][:, 3, :], m == 0, m == MC - 1)
                last.then_inc(down_done, 1)

            def feed_forward(n, last_block=False, begun=0):
                for m in range(MC):
                    if m >= begun:
                        up(n, m)
                    if 0 < m < MC - 1:
                        down(n, m - 1)
                for t in range(TILES):
                    if not last_block:
                        job_steps(n * TILES + (FFN_JOB + t), TURN_BANK[t % 2],
                                  n * TILES + (FFN_JOB + (0 if t < 2 else t - 1)), "x", t, 0, KC,
                                  ready=n * TILES + (TILES * (NB + 1) + t + 1))
                    if t == 1:
                        down(n, MC - 2)
                down(n, MC - 1)
                if not last_block:
                    pe.wait_ge(job_out, n * TILES + (FFN_JOB + TILES))

            end = Block(PAIRS, 0)
            for u in range(-LAG, 0):
                turn(*end.unit(u))
            p_v(end.prev(), GROUPS - 1)
            pe.wait_ge(masked, UNITS * NB)
            up(0, 0)
            pe.wait_ge(oT_ready, GROUPS * NB)
            for t in range(TILES):
                job_steps(O_LAST + t, JOB_BANK[(O_LAST + t) % 3], O_LAST + t - 2, "o", t, 0, KC, end)
            pe.wait_ge(pT_ready, UNITS * NB)
            pe.wait_ge(job_out, FFN_JOB)
            feed_forward(0, begun=1)
            with pe.Fori(1, NB - 1) as n:
                feed_forward(n)
            feed_forward(NB - 1, last_block=True)

        @block.scalar
        def _(act):
            act.dma_start(bk_col[:], bk).then_inc(in_cols, 16)
            act.dma_start(bq_col[:], bq).then_inc(in_cols, 16)
            act.dma_start(b1_col[:], b1).then_inc(in_cols, 16)
            act.dma_start(wq_raw[:], rows(wqT)).then_inc(in_wq, 16)
            act.dma_start(wv_raw[:], rows(wvT)).then_inc(in_v, 16)
            act.dma_start(bv_row[:], bv.to_broadcast([P, D])).then_inc(in_rows, 16)
            act.dma_start(bo_row[:], bo.to_broadcast([P, D])).then_inc(in_rows, 16)
            act.dma_start(wo_raw[:], rows(woT)).then_inc(in_wo, 16)
            act.dma_start(b2_row[:], b2.to_broadcast([P, D])).then_inc(in_rows, 16)

            def x_hi(job, src, t):
                act.wait_ge(job_done, job + 1)
                act.activation(xT_hi[:, :, t * P:(t + 1) * P], src[:, :].rearrange("p (k j) -> p k j", j=P),
                               ACT.Copy).then_inc(job_hi, 1)

            def q_hi(job, src, c, units):
                act.wait_ge(job_done, job + 1)
                wait(act, scored, units)
                act.activation(qT_hi[:, c % 2, :], src[:, :], ACT.Identity,
                               bias=bq_col[:, c:c + 1]).then_inc(job_hi, 1)

            def pT_out(blk, u):
                c, t = divmod(u, TILES)
                act.wait_ge(turned, blk.at(UNITS, u + 1))
                if t == 0:
                    wait(act, pv_done, blk.at(GROUPS, c - 1))
                    if blk.first and c == 0:
                        act.wait_ge(v_done, B)
                act.activation(pT[:, c % 2, :, t * P:(t + 1) * P],
                               T_BANK[u % 2][:, :].rearrange("p (h j) -> p h j", j=P), ACT.Copy).then_inc(pT_ready, 1)

            def exps(blk, u):
                t = u % TILES
                act.wait_ge(maxed, blk.at(UNITS, u + 1))
                wait(act, turned, blk.at(UNITS, u - 3))
                for j in range(4):
                    last = act.activation(pr[:, t, j, :], sc[:, t, j, :], ACT.Exp, bias=neg_max[:, t, j:j + 1],
                                          accum_out=row_sum[:, t, j:j + 1])
                last.then_inc(exped, 1)

            def oT_out(blk, c):
                act.wait_ge(pv_done, blk.at(GROUPS, c + 1))
                if blk.first and c == 0:
                    act.wait_ge(v_ready, B)
                act.activation(oT_hi[:, blk.batch, c, :], PV_BANK[:, :], ACT.Copy).then_inc(oT_hi_done, 1)

            for t in range(TILES):
                x_hi(t, JOB_BANK[t % 3], t)
            act.wait_ge(in_cols, 48)
            q_hi(TILES, JOB_BANK[TILES % 3], 0, 0)
            act.wait_ge(kv_step, KV_STEPS)

            def attention(blk):
                for u in range(UNITS):
                    if not (blk.first and u < LAG):
                        pT_out(*blk.unit(u - LAG))
                    exps(blk, u)
                    for kind, which, job, _, n in blk.jobs(u):
                        if kind == "x":
                            x_hi(job, JOB_BANK[n], which)
                        elif kind == "q":
                            q_hi(job, JOB_BANK[n], which, blk.at(UNITS, TILES * (which - 1)))
                        elif kind == "q0":
                            q_hi(job, JOB_BANK[n], 0, blk.at(UNITS, TILES * (GROUPS - 1)))
                    if blk.pv(u):
                        oT_out(*blk.pv(u))

            all_pairs(act, attention)
            end = Block(PAIRS, 0)
            for u in range(-LAG, 0):
                pT_out(*end.unit(u))
            oT_out(end.prev(), GROUPS - 1)

            def feed_forward(n, last_block=False):
                for m in range(MC):
                    g = n * MC + m
                    act.wait_ge(up_done, g + 1)
                    wait(act, h_ready, g - 1)
                    act.activation(h_raw[:, m % 2, :], UP_BANK[m % 2][:, :], ACT.Relu,
                                   bias=b1_col[:, m:m + 1]).then_inc(relued, 1)
                if not last_block:
                    for t in range(TILES):
                        x_hi(n * TILES + (FFN_JOB + t), TURN_BANK[t % 2], t)

            feed_forward(0)
            with act.Fori(1, NB - 1) as n:
                feed_forward(n)
            feed_forward(NB - 1, last_block=True)

        @block.vector
        def _(dve):
            def count(t, ready):
                dve.wait_ge(in_x[t], ready)
                dve.bn_stats(stats[:, t, :], xn[:, t, :]).then_inc(counted, 1)

            def mean(done, t):
                dve.wait_ge(counted, done + 1)
                wait(dve, normed, done - t)
                dve.sem_inc(passed, 1)
                dve.bn_aggr(mean_var[:, t, :], stats[:, t, :]).then_inc(meaned, 1)

            def normalise(t, ready):
                dve.wait_ge(rstd_ready, ready)
                dve.tensor_scalar(xn[:, t, :], xn[:, t, :], mean_var[:, t, 0:1], rstd[:, t:t + 1],
                                  ALU.subtract, ALU.mult).then_inc(normed, 1)

            def x_lo(hi_no, src, t):
                dve.wait_ge(job_hi, hi_no + 1)
                tok = slice(t * P, (t + 1) * P)
                dve.tensor_tensor(xT_lo[:, :, tok], src[:, :].rearrange("p (k j) -> p k j", j=P),
                                  xT_hi[:, :, tok].bitcast(F32), ALU.subtract).then_inc(job_out, 1)

            def q_lo(hi_no, src, c):
                dve.wait_ge(job_hi, hi_no + 1)
                dve.scalar_tensor_tensor(out=qT_lo[:, c % 2, :], in0=src[:, :], scalar=bq_col[:, c:c + 1],
                                         in1=qT_hi[:, c % 2, :].bitcast(F32), op0=ALU.add,
                                         op1=ALU.subtract).then_inc(job_out, 1)

            def x2_sum(job, src, t, ready):
                dve.wait_ge(job_done, job + 1)
                dve.wait_ge(biased, ready)
                dve.tensor_tensor(res[:, t, :], src[:, :], res[:, t, :], ALU.add).then_inc(job_out, 1)

            def oT_low(blk, c):
                dve.wait_ge(oT_hi_done, blk.at(GROUPS, c + 1))
                dve.tensor_tensor(oT_lo[:, blk.batch, c, :], PV_BANK[:, :],
                                  oT_hi[:, blk.batch, c, :].bitcast(F32), ALU.subtract).then_inc(oT_ready, 1)

            dve.memset(kbd_lo[:].bitcast(F32), 0.0).then_inc(kv_step, 1)
            for t in range(TILES):
                count(t, 16)
                mean(t, t)
            for t in range(TILES):
                normalise(t, 1)
            dve.wait_ge(in_wq, 16)
            dve.tensor_copy(wq_hi[:], wq_raw[:]).then_inc(wq_step, 1)
            for t in range(TILES):
                x_lo(t, JOB_BANK[t % 3], t)
            dve.wait_ge(wq_step, 1)
            dve.tensor_tensor(wq_lo[:], wq_raw[:], wq_hi[:].bitcast(F32), ALU.subtract).then_inc(wq_step, 1)
            dve.wait_ge(in_cols, 48)
            for c in range(GROUPS):
                dve.wait_ge(k_done, c + 1)
                last = dve.tensor_scalar(k_raw[:, c], bank[c][:, 0:B * KEYS].rearrange("p (b k) -> p b k", b=B),
                                         bk_col[:, c:c + 1], float(DK) ** -0.5, ALU.add, ALU.mult)
                last.then_inc(kv_step, 1)
            dve.wait_ge(kv_step, 1 + GROUPS)
            dve.wait_ge(made, 2)

            def head(t, j):
                return t[j * DK:(j + 1) * DK, :, :, j * KEYS:(j + 1) * KEYS]

            def k_head(j):
                return k_raw[j * DK:(j + 1) * DK].rearrange("p c b k -> p b c k")

            for j in range(4):
                dve.tensor_copy(head(kbd_hi, j), k_head(j)).then_inc(kv_step, 1)
            q_lo(TILES, JOB_BANK[TILES % 3], 0)
            for j in range(4):
                dve.wait_ge(kv_step, 1 + GROUPS + j + 1)
                dve.tensor_tensor(head(kbd_lo, j), k_head(j), head(kbd_hi, j).bitcast(F32),
                                  ALU.subtract).then_inc(kv_step, 1)

            def v_out(b):
                dve.wait_ge(v_done, b + 1)
                dve.tensor_tensor(v_sb[:, b, :], PV_BANK[:, :], bv_row[:], ALU.add).then_inc(v_ready, 1)

            def late(blk, u):
                for kind, which, job, hi_no, n in blk.jobs(u):
                    if kind == "x":
                        x_lo(hi_no, JOB_BANK[n], which)
                    elif kind == "o":
                        x2_sum(job, JOB_BANK[n], which, blk.at(TILES, which + 1 - TILES))
                    else:
                        q_lo(hi_no, JOB_BANK[n], which)
                if blk.first and u in V_SLOTS:
                    if u == min(V_SLOTS):
                        dve.wait_ge(in_rows, 48)
                    v_out(V_SLOTS[u])
                if blk.pv(u):
                    oT_low(*blk.pv(u))

            def invert(blk, u):
                t = u % TILES
                dve.wait_ge(exped, blk.at(UNITS, u + 1))
                wait(dve, scaled, blk.at(UNITS, u - 3))
                dve.reciprocal(row_inv[:, t, :], row_sum[:, t, :]).then_inc(inverted, 1)

            def attention(blk):
                for u in range(UNITS):
                    c, t = divmod(u, TILES)
                    dve.wait_ge(scored, blk.at(UNITS, u + 1))
                    wait(dve, exped, blk.at(UNITS, u - 3))
                    if c == 0:
                        dve.wait_ge(filled, blk.at(TILES, t + 1))
                    if u == 0:
                        dve.wait_ge(in_mask[blk.b], blk.i * 16 + 16)
                    dve.sem_inc(passed, 1)
                    dve.copy_predicated(sc[:, t], mask_sb[:, blk.b, t, :].unsqueeze(1).to_broadcast([P, 4, KEYS]),
                                        S_BANK[u % 2][:, :].rearrange("p (h k) -> p h k", k=KEYS)).then_inc(masked, 1)
                    if u in STATS_SLOTS:
                        count(STATS_SLOTS[u], blk.at(16, 32))
                    if not (blk.first and u == 0):
                        invert(*blk.unit(u - 1))
                    dve.wait_ge(masked, blk.at(UNITS, u + 1))
                    dve.tensor_reduce(neg_max[:, t, :], sc[:, t], AX.X, ALU.max, negate=True).then_inc(maxed, 1)
                    if u in STATS_SLOTS:
                        mean(blk.at(TILES, TILES + STATS_SLOTS[u]), STATS_SLOTS[u])
                    if not (blk.first and u == 0):
                        late(*blk.unit(u - 1))
                    if u in APPLY_SLOTS:
                        normalise(APPLY_SLOTS[u], blk.at(1, 2))

            all_pairs(dve, attention)
            end = Block(PAIRS, 0)
            invert(*end.unit(-1))
            late(Block(PAIRS - 1, 1, last=True), UNITS - 1)
            oT_low(end.prev(), GROUPS - 1)
            for t in range(TILES):
                x2_sum(O_LAST + t, JOB_BANK[(O_LAST + t) % 3], t, TILES * (NB - 1) + t + 1)

            def feed_forward(n, last_block=False):
                for m in range(MC):
                    g = n * MC + m
                    dve.wait_ge(relued, g + 1)
                    wait(dve, down_done, g - 1)
                    dve.tensor_copy(h_hi[:, m % 2, :], h_raw[:, m % 2, :]).then_inc(hi_done, 1)
                    if 2 <= m < 2 + TILES and not last_block:
                        count(m - 2, n * 16 + 16 * (NB + 2))
                    dve.wait_ge(hi_done, g + 1)
                    dve.tensor_tensor(h_lo[:, m % 2, :], h_raw[:, m % 2, :], h_hi[:, m % 2, :].bitcast(F32),
                                      ALU.subtract).then_inc(h_ready, 1)
                    if 2 <= m < 2 + TILES and not last_block:
                        mean(n * TILES + (TILES * (NB + 1) + m - 2), m - 2)
                    if MC - 1 - TILES <= m < MC - 1 and not last_block:
                        normalise(m - (MC - 1 - TILES), n + (NB + 2))
                if not last_block:
                    for t in range(TILES):
                        x_lo(n * TILES + (FFN_HI + t), TURN_BANK[t % 2], t)
                for t in range(TILES):
                    dve.wait_ge(down_done, n * MC + MC)
                    dve.wait_ge(biased, n * TILES + (TILES * NB + t + 1))
                    dve.tensor_tensor(res[:, t, :], ACC_BANK[t][:, :], res[:, t, :], ALU.add).then_inc(summed, 1)

            feed_forward(0)
            with dve.Fori(1, NB - 1) as n:
                feed_forward(n)
            feed_forward(NB - 1, last_block=True)

        @block.gpsimd
        def _(pool):
            def split(raw, hi, lo, sem_, before):
                pool.tensor_scalar(hi, raw, 1.0, 0.0, ALU.mult, ALU.add).then_inc(sem_, 1)
                pool.wait_ge(sem_, before + 1)
                pool.tensor_tensor(lo, raw, hi.bitcast(F32), ALU.subtract).then_inc(sem_, 1)

            def rstds(ready):
                pool.wait_ge(meaned, ready * TILES)
                pool.tensor_tensor(rstd[:], mean_var[:, :, 1], eps[:], ALU.add).then_inc(eps_added, 1)
                pool.wait_ge(eps_added, ready)
                pool.tensor_tensor(rstd[:], rstd[:], minus_half[:], ALU.pow).then_inc(rstd_ready, 1)

            def add_bias(t, landed, row):
                pool.wait_ge(in_res[t], landed)
                pool.tensor_tensor(res[:, t, :], res[:, t, :], row[:], ALU.add).then_inc(biased, 1)

            def fill(t):
                pool.memset(sc[:, t], MASKED).then_inc(filled, 1)

            def scale(blk, u):
                t = u % TILES
                pool.wait_ge(inverted, blk.at(UNITS, u + 1))
                pool.tensor_tensor(pr[:, t], pr[:, t], row_inv[:, t, :].unsqueeze(2).to_broadcast([P, 4, KEYS]),
                                   ALU.mult).then_inc(scaled, 1)

            pool.memset(minus_half[:], -0.5).then_inc(zeroed, 1)
            pool.memset(eps[:], EPS).then_inc(zeroed, 1)
            pool.memset(ident[:], 0.0).then_inc(zeroed, 1)
            pool.wait_ge(zeroed, 3)
            pool.affine_select(out=ident[:], in_=ident[:], compare_op=ALU.not_equal, fill=1.0, base=0,
                               pattern=[[-1, P]], channel_multiplier=1).then_inc(made, 1)
            pool.memset(kbd_hi[:].bitcast(F32), 0.0).then_inc(made, 1)
            rstds(1)
            for t in range(TILES):
                fill(t)
            pool.wait_ge(in_wo, 16)
            split(wo_raw[:], wo_hi[:], wo_lo[:], wo_step, 0)
            pool.wait_ge(in_rows, 48)

            def attention(blk):
                for u in range(UNITS):
                    if not (blk.first and u == 0):
                        scale(*blk.unit(u - 1))
                    if u > UNITS - TILES and not blk.last:
                        fill(u - 1 - (UNITS - TILES))
                    if u == 0 and not blk.first:
                        fill(TILES - 1)
                    if u == RSTD_SLOT:
                        rstds(blk.at(1, 2))
                    if u in BIAS_SLOTS and not blk.first:
                        add_bias(BIAS_SLOTS[u], blk.at(16), bo_row)

            all_pairs(pool, attention)
            scale(*Block(PAIRS, 0).unit(-1))
            for t in range(TILES):
                add_bias(t, 16 * NB, bo_row)

            for m in range(MC):
                if m == 0:
                    pool.wait_ge(scored, UNITS * NB)
                if m == early_chunks:
                    pool.wait_ge(job_done, FFN_JOB)
                pool.wait_ge(in_w[m % STAGE], 32 * (m // STAGE + 1))
                for part in range(2):
                    split(w_stage[:, m % STAGE, part, :], w_chunk[m][:, 2 * part, :], w_chunk[m][:, 2 * part + 1, :],
                          w_step, 4 * m + 2 * part)

            def feed_forward(n, last_block=False):
                for t in range(TILES):
                    add_bias(t, n * 16 + 16 * (NB + 1), b2_row)
                if not last_block:
                    rstds(n + (NB + 2))

            feed_forward(0)
            with pool.Fori(1, NB - 1) as n:
                feed_forward(n)
            feed_forward(NB - 1, last_block=True)


def kernel(x, ctx_1024, mask_Bx1xSxS2_ik0, L0_xattn_Wq, L0_xattn_bq, L0_xattn_Wk, L0_xattn_bk, L0_xattn_Wv,
           L0_xattn_bv, L0_xattn_Wo, L0_xattn_bo, L0_ffn_W1, L0_ffn_b1, L0_ffn_W2, L0_ffn_b2):
    import numpy as np
    import concourse.bacc as bacc
    from concourse.bass_utils import run_bass_kernel_spmd

    lay = np.ascontiguousarray
    x, ctx, mask = np.asarray(x), np.asarray(ctx_1024), np.asarray(mask_Bx1xSxS2_ik0)
    arrays = {
        "x": lay(x.reshape(B * S, D)),
        "ctxT": lay(ctx.reshape(B * KEYS, D).T),
        "mask": lay(mask.reshape(B * S, KEYS)),
        "wqT": lay(np.asarray(L0_xattn_Wq).T), "bq": lay(np.asarray(L0_xattn_bq).reshape(KC, P).T),
        "wkT": lay(np.asarray(L0_xattn_Wk).T), "bk": lay(np.asarray(L0_xattn_bk).reshape(KC, P).T),
        "wvT": lay(np.asarray(L0_xattn_Wv).T), "bv": lay(np.asarray(L0_xattn_bv).reshape(1, D)),
        "woT": lay(np.asarray(L0_xattn_Wo).T), "bo": lay(np.asarray(L0_xattn_bo).reshape(1, D)),
        "w1": lay(np.asarray(L0_ffn_W1)), "b1": lay(np.asarray(L0_ffn_b1).reshape(MC, P).T),
        "w2": lay(np.asarray(L0_ffn_W2)), "b2": lay(np.asarray(L0_ffn_b2).reshape(1, D)),
    }
    nc = bacc.Bacc("TRN2", target_bir_lowering=False, num_devices=1)
    args = [nc.dram_tensor(f"in_{name}", a.shape, mybir.dt.from_np(a.dtype), kind="ExternalInput").ap()
            for name, a in arrays.items()]
    x2 = nc.dram_tensor("x2_between", (B * S, D), F32, kind="Internal").ap()
    out = nc.dram_tensor("out_0", (B * S, D), F32, kind="ExternalOutput").ap()
    build(nc, *args, x2, out)
    r = run_bass_kernel_spmd(nc, [{f"in_{name}": a for name, a in arrays.items()}], core_ids=[0])
    return r.results[0]["out_0"].reshape(B, S, D)
```

```python
from contextlib import ExitStack

import concourse.bass as bass
from concourse import mybir

F32 = mybir.dt.float32
F32R = mybir.dt.float32r
I32 = mybir.dt.int32
ALU = mybir.AluOpType
ACT = mybir.ActivationFunctionType
AX = mybir.AxisListType

P = 128
B = 2
S = 2048
D = 512
KEYS = 128
H = 16
DK = D // H
INTER = 2048
BLOCK = 512
TILES = BLOCK // P
NB = B * S // BLOCK
PAIRS = NB // B
KC = D // P
GROUPS = H // 4
UNITS = GROUPS * TILES
MC = INTER // P
WARM_UP = 52
LAG = 3
STAGE = 3
EPS = 1e-5
MASKED = -1000000000.0

STEPS = {
    0: [], 1: [("q", 1, 0, 4)], 2: [("q", 2, 0, 1)], 3: [("q", 2, 1, 3)], 4: [("q", 2, 3, 4), ("o", 1, 0, 1)],
    5: [], 6: [("o", 0, 0, 2), ("o", 1, 1, 2), ("o", 0, 2, 4)], 7: [("q", 3, 0, 2)], 8: [("o", 1, 2, 4)],
    9: [("q", 3, 2, 4), ("x", 0, 0, 4)], 10: [("x", 1, 0, 4)], 11: [("x", 2, 0, 4), ("x", 3, 0, 4)],
    12: [("o", 2, 0, 2)],
    13: [("o", 2, 2, 3), ("q0", 0, 0, 2), ("o", 2, 3, 4), ("q0", 0, 2, 3), ("o", 3, 0, 1), ("q0", 0, 3, 4)],
    14: [("o", 3, 1, 4)], 15: [],
}
W_SLOTS = {10: 0, 11: 1, 12: 2, 13: 3, 14: 4, 15: 5}
JOBS = [(slot, kind, which) for slot in range(UNITS) for kind, which, _, end in STEPS[slot] if end == KC]
PV_SLOTS = {3: 3, 7: 0, 11: 1, 15: 2}
STATS_SLOTS = {0: 0, 1: 1, 2: 2, 3: 3}
RSTD_SLOT = 5
APPLY_SLOTS = {6: 0, 7: 1, 8: 2, 9: 3}
BIAS_SLOTS = {1: 0, 4: 1, 7: 2, 8: 3}
K_SLOTS = {2: 3}
K_OUT_SLOTS = {0: 2, 2: 3}
KBD_HI_SLOTS = {1: 2, 3: 3}
KBD_LOW_SLOTS = {0: 1, 4: 2, 8: 3}
V_SLOTS = {5: 0, 9: 1}
WO_SLOTS = {6 + n: n for n in range(2 * KC)}
N_PRO = TILES + 1


class Block:

    def __init__(self, i, b, first=False, last=False):
        self.i, self.b, self.first, self.last = i, b, first, last
        self.batch = b % B

    def prev(self):
        return Block(self.i, self.b - 1, first=isinstance(self.i, int) and 2 * self.i + self.b == 1)

    def unit(self, u):
        return (self, u) if u >= 0 else (self.prev(), u + UNITS)

    def at(self, per, k=0):
        return self.i * (2 * per) + (self.b * per + k)

    def has(self, kind):
        return not (kind == "o" and self.first) and not (kind == "q0" and self.last)

    def held(self, kind, which):
        return self.last and (kind, which) == ("o", TILES - 1)

    def jobs(self, slot=None):
        out, j, h = [], 0, 0
        for s, kind, which in JOBS:
            if self.has(kind):
                if slot is None or s == slot:
                    job = N_PRO + j if self.first else self.at(len(JOBS), N_PRO - TILES + j)
                    out.append((kind, which, job, self.at(len(JOBS) - TILES, N_PRO + h),
                                (N_PRO + j - (0 if self.first else TILES)) % 3))
                j += 1
                h += kind != "o"
        return out

    def job(self, kind, which=0):
        return next(x[2] for x in self.jobs() if x[:2] == (kind, which))

    def bank(self, kind, which=0):
        return next(x[4] for x in self.jobs() if x[:2] == (kind, which))

    def q_ready(self, c):
        if c:
            return self.job("q", c) + 1
        return N_PRO if self.first else self.prev().job("q0") + 1

    def pv(self, slot):
        c = PV_SLOTS.get(slot)
        if c is None or (c == 3 and self.first):
            return None
        return (self.prev(), c) if c == 3 else (self, c)


assert JOBS[-1][1:] == ("o", TILES - 1)
O_LAST = N_PRO + len(JOBS) * NB - TILES - 1
FFN_JOB = O_LAST + TILES
FFN_HI = N_PRO + (len(JOBS) - TILES) * NB - 1


def wait(eng, sem, value):
    if not isinstance(value, int) or value > 0:
        eng.wait_ge(sem, value)


def build(nc, x, ctxT, mask, wqT, bq, wkT, bk, wvT, bv, woT, bo, w1, b1, w2, b2, x2_dram, out):
    ctx = ExitStack()
    with ctx:
        base = -(-nc.sbuf_base // 64) * 64
        top = [base]

        def sb(name, shape, dt=F32, at=None):
            size = 4
            for n in shape[1:]:
                size *= n
            where = top[0] if at is None else at
            if at is None:
                top[0] += -(-size // 64) * 64
            t = nc.alloc_sbuf_tensor_at(name, shape, dt, offset=where)
            return t

        ident = sb("ident", [P, P])
        minus_half = sb("minus_half", [P, TILES])
        eps = sb("eps", [P, TILES])
        bo_row = sb("bo_row", [P, D])
        b2_row = sb("b2_row", [P, D])
        bq_col = sb("bq_col", [P, KC])
        bk_col = sb("bk_col", [P, KC])
        b1_col = sb("b1_col", [P, MC])
        stats = sb("stats", [P, TILES, 6])
        mean_var = sb("mean_var", [P, TILES, 2])
        rstd = sb("rstd", [P, TILES])
        neg_max = sb("neg_max", [P, TILES, 4])
        row_sum = sb("row_sum", [P, TILES, 4])
        row_inv = sb("row_inv", [P, TILES, 4])
        xn = sb("xn", [P, TILES, D])
        res = sb("res", [P, TILES, D])
        xT_hi = sb("xT_hi", [P, KC, BLOCK], F32R)
        xT_lo = sb("xT_lo", [P, KC, BLOCK], F32R)
        stage_at = top[0]
        h_raw = sb("h_raw", [P, 2, BLOCK])
        h_hi = sb("h_hi", [P, 2, BLOCK], F32R)
        h_lo = sb("h_lo", [P, 2, BLOCK], F32R)
        w_stage = sb("w_stage", [P, STAGE, 2, D])
        ffn_at = top[0]
        wq_hi = sb("wq_hi", [P, KC, D], F32R)
        wq_lo = sb("wq_lo", [P, KC, D], F32R)
        q_free = top[0]
        kbd_hi = sb("kbd_hi", [P, B, GROUPS, 4 * KEYS], F32R)
        kbd_lo = sb("kbd_lo", [P, B, GROUPS, 4 * KEYS], F32R)
        qT_hi = sb("qT_hi", [P, 2, BLOCK], F32R)
        qT_lo = sb("qT_lo", [P, 2, BLOCK], F32R)
        early_free = top[0]
        wo_hi = sb("wo_hi", [P, KC, D], F32R)
        wo_lo = sb("wo_lo", [P, KC, D], F32R)
        v_sb = sb("v_sb", [P, B, D])
        oT_at = top[0]
        oT_hi = sb("oT_hi", [P, 2, GROUPS, BLOCK], F32R)
        oT_lo = sb("oT_lo", [P, 2, GROUPS, BLOCK], F32R)
        sc = sb("sc", [P, TILES, 4, KEYS])
        pr = sb("pr", [P, TILES, 4, KEYS])
        pT_at = top[0]
        pT = sb("pT", [P, 2, 4, BLOCK])
        mask_sb = sb("mask_sb", [P, 2, TILES, KEYS], I32)
        end_a = top[0]
        chunk_bytes = 4 * D * 4
        q_chunks = (q_free - ffn_at) // chunk_bytes
        early_chunks = (early_free - ffn_at) // chunk_bytes
        w_chunk = [sb(f"w_chunk{m}", [P, 4, D], F32R, at=ffn_at + m * chunk_bytes) for m in range(MC)]
        assert max(end_a, ffn_at + MC * chunk_bytes) <= nc.sbuf_usable_end
        wq_raw = sb("wq_raw", [P, KC, D], at=stage_at)
        wo_raw = sb("wo_raw", [P, KC, D], at=stage_at + 4 * KC * D)
        wk_raw = sb("wk_raw", [P, KC, D], at=pT_at)
        ctx_raw = sb("ctx_raw", [P, KC, B * KEYS], at=oT_at + 4 * GROUPS * BLOCK)
        k_raw = sb("k_raw", [P, GROUPS, B, KEYS], at=oT_at + 4 * GROUPS * BLOCK + 4 * KC * B * KEYS)
        wv_raw = sb("wv_raw", [P, KC, D], at=oT_at + 3 * 4 * GROUPS * BLOCK)
        bv_row = sb("bv_row", [P, D], at=stage_at + 8 * KC * D)

        bank = [ctx.enter_context(nc.psum_tensor(f"bank{n}", [P, 512], F32)) for n in range(8)]
        S_BANK, T_BANK, PV_BANK, JOB_BANK = bank[0:2], bank[2:4], bank[4], bank[5:8]
        K_BANK = bank[0:3] + [PV_BANK]
        UP_BANK, ACC_BANK, TURN_BANK = bank[0:2], bank[2:6], bank[6:8]

        def sem(name):
            return ctx.enter_context(nc.semaphore(name))

        in_x = [sem(f"in_x{t}") for t in range(TILES)]
        in_res = [sem(f"in_res{t}") for t in range(TILES)]
        stored = [sem(f"stored{t}") for t in range(TILES)]
        in_mask = [sem(f"in_mask{b}") for b in range(B)]
        in_k, in_v, in_bv, in_wq, in_wo = sem("in_k"), sem("in_v"), sem("in_bv"), sem("in_wq"), sem("in_wo")
        in_rows, in_cols = sem("in_rows"), sem("in_cols")
        in_w = [sem(f"in_w{r}") for r in range(STAGE)]
        k_done, v_done = sem("k_done"), sem("v_done")
        scored = sem("scored")
        turned = sem("turned")
        pv_done = sem("pv_done")
        job_done = sem("job_done")
        up_done = sem("up_done")
        down_done = sem("down_done")
        wq_hi_done = sem("wq_hi_done")
        kbd_first_hi = sem("kbd_first_hi")
        exped = sem("exped")
        pT_ready = sem("pT_ready")
        job_hi = sem("job_hi")
        oT_hi_done = sem("oT_hi_done")
        relued = sem("relued")
        k_ready = sem("k_ready")
        kbd_ready = sem("kbd_ready")
        v_ready = sem("v_ready")
        wq_ready = sem("wq_ready")
        masked = sem("masked")
        maxed = sem("maxed")
        inverted = sem("inverted")
        job_out = sem("job_out")
        oT_ready = sem("oT_ready")
        counted = sem("counted")
        meaned = sem("meaned")
        normed = sem("normed")
        hi_done = sem("hi_done")
        h_ready = sem("h_ready")
        summed = sem("summed")
        passed = sem("passed")
        zeroed = sem("zeroed")
        made = sem("made")
        kbd_hi_done = sem("kbd_hi_done")
        filled = sem("filled")
        scaled = sem("scaled")
        eps_added = sem("eps_added")
        rstd_ready = sem("rstd_ready")
        biased = sem("biased")
        wq_split = sem("wq_split")
        wo_step = sem("wo_step")
        w_step = sem("w_step")

        x_v = x.rearrange("(b i t p) d -> b i t p d", b=B, i=PAIRS, t=TILES)
        mask_v = mask.rearrange("(b i t p) k -> b i p t k", b=B, i=PAIRS, t=TILES)
        x2_v = x2_dram.rearrange("(b i t p) d -> b i t p d", b=B, i=PAIRS, t=TILES)
        x2_n = x2_dram.rearrange("(n t p) d -> n t p d", n=NB, t=TILES)
        out_n = out.rearrange("(n t p) d -> n t p d", n=NB, t=TILES)
        w1_v = w1.rearrange("(k p) (m j) -> m p k j", p=P, j=P)
        w2_v = w2.rearrange("(m p) d -> m p d", p=P)

        def rows(w):
            return w.rearrange("(k p) n -> p k n", p=P)

        blocks_first = [Block(0, 0, first=True), Block(0, 1)]
        blocks_last = [Block(PAIRS - 1, 0), Block(PAIRS - 1, 1, last=True)]

        def all_pairs(eng, run):
            for blk in blocks_first:
                run(blk)
            with eng.Fori(1, PAIRS - 1) as i:
                for b in range(B):
                    run(Block(i, b))
            for blk in blocks_last:
                run(blk)

        def head(t, j, c):
            return t[j * DK:(j + 1) * DK, :, c, j * KEYS:(j + 1) * KEYS]

        def k_head(j, c):
            return k_raw[j * DK:(j + 1) * DK, c]

        block = ctx.enter_context(nc.Block())

        @block.sync
        def _(sp):
            for t in range(TILES):
                sp.dma_start(xn[:, t, :], x_v[0, 0, t]).then_inc(in_x[t], 16)
            sp.dma_start(ctx_raw[:], rows(ctxT)).then_inc(in_k, 16)
            sp.dma_start(wk_raw[:], rows(wkT)).then_inc(in_k, 16)
            sp.dma_start(wq_raw[:], rows(wqT)).then_inc(in_wq, 16)
            sp.dma_start(mask_sb[:, 0], mask_v[0, 0]).then_inc(in_mask[0], 16)
            sp.dma_start(wv_raw[:], rows(wvT)).then_inc(in_v, 16)
            sp.dma_start(bv_row[:], bv.to_broadcast([P, D])).then_inc(in_bv, 16)
            for t in range(TILES):
                sp.wait_ge(job_done, t + 1)
                sp.dma_start(xn[:, t, :], x_v[1, 0, t]).then_inc(in_x[t], 16)
            sp.dma_start(wo_raw[:], rows(woT)).then_inc(in_wo, 16)
            for t in range(TILES):
                sp.dma_start(res[:, t, :], x_v[0, 0, t]).then_inc(in_res[t], 16)
            sp.dma_start(bo_row[:], bo.to_broadcast([P, D])).then_inc(in_rows, 16)
            sp.dma_start(b2_row[:], b2.to_broadcast([P, D])).then_inc(in_rows, 16)

            def load_chunk(m):
                r = m % STAGE
                sp.dma_start(w_stage[:, r, 0, :].rearrange("p (k j) -> p k j", j=P), w1_v[m]).then_inc(in_w[r], 16)
                sp.dma_start(w_stage[:, r, 1, :], w2_v[m]).then_inc(in_w[r], 16)

            def attention(blk):
                b, last_pair = blk.b, isinstance(blk.i, int) and blk.i == PAIRS - 1

                def store(t):
                    sp.wait_ge(job_out, blk.job("o", t) + 1)
                    sp.dma_start(x2_v[1 - b, blk.i - (1 - b), t], res[:, t, :]).then_inc(stored[t], 16)

                def residual(t):
                    sp.wait_ge(stored[t], blk.at(16))
                    sp.dma_start(res[:, t, :], x_v[b, blk.i, t]).then_inc(in_res[t], 16)

                if not blk.last:
                    wait(sp, masked, blk.at(UNITS))
                    sp.dma_start(mask_sb[:, 1 - b], mask_v[1 - b, blk.i + b]).then_inc(in_mask[1 - b], 16)
                if blk.last:
                    sp.wait_ge(wq_ready, KC // 2)
                    sp.wait_ge(wq_split, KC)
                    sp.wait_ge(wo_step, 2 * KC)
                    sp.wait_ge(v_ready, B)
                    for m in range(STAGE):
                        load_chunk(m)
                if not blk.first:
                    store(0)
                    store(1)
                for t in range(TILES):
                    sp.wait_ge(job_done, blk.job("x", t) + 1)
                    src = x2_n[b, t] if last_pair else x_v[b, blk.i + 1, t]
                    sp.dma_start(xn[:, t, :], src).then_inc(in_x[t], 16)
                if not blk.first:
                    residual(0)
                    residual(1)
                    store(2)
                    residual(2)
                    store(3)
                    residual(3)

            all_pairs(sp, attention)

            for m in range(STAGE, 2 * STAGE):
                sp.wait_ge(w_step, 4 * (m - STAGE + 1))
                load_chunk(m)
                if m < 2 * STAGE - 1:
                    for t in range(2 * (m - STAGE), 2 * (m - STAGE) + 2):
                        sp.wait_ge(job_out, O_LAST + t + 1)
                        sp.dma_start(x2_v[B - 1, PAIRS - 1, t], res[:, t, :]).then_inc(stored[t], 16)
            for t in range(TILES):
                sp.wait_ge(stored[t], 16 * NB)
                sp.dma_start(res[:, t, :], x2_n[0, t]).then_inc(in_res[t], 16)
            for m in range(2 * STAGE, MC):
                sp.wait_ge(w_step, 4 * (m - STAGE + 1))
                load_chunk(m)

            def store_and_reload(n, reload_res, reload_x):
                if reload_x:
                    for t in range(TILES):
                        sp.wait_ge(job_done, n * TILES + (FFN_JOB + t + 1))
                        sp.dma_start(xn[:, t, :], x2_n[n + 2, t]).then_inc(in_x[t], 16)
                for t in range(TILES):
                    sp.wait_ge(summed, n * TILES + (t + 1))
                    sp.dma_start(out_n[n, t], res[:, t, :]).then_inc(stored[t], 16)
                if reload_res:
                    for t in range(TILES):
                        sp.wait_ge(stored[t], n * 16 + 16 * (NB + 1))
                        sp.dma_start(res[:, t, :], x2_n[n + 1, t]).then_inc(in_res[t], 16)

            with sp.Fori(0, NB - 2) as n:
                store_and_reload(n, True, True)
            store_and_reload(NB - 2, True, False)
            store_and_reload(NB - 1, False, False)
            for t in range(TILES):
                sp.wait_ge(stored[t], 16 * 2 * NB)

        @block.tensor
        def _(pe):
            def three(out_ap, a_hi, a_lo, b_hi, b_lo, start, stop):
                pe.matmul(out_ap, a_lo, b_hi, start=start, stop=False)
                pe.matmul(out_ap, a_hi, b_lo, start=False, stop=False)
                return pe.matmul(out_ap, a_hi, b_hi, start=False, stop=stop)

            def job_steps(job, dst, free, kind, which, k0, k1, blk=None, ready=None):
                if k0 == 0:
                    wait(pe, job_out, free)
                    if kind == "x":
                        pe.wait_ge(normed, ready)
                tok = slice(which * P, (which + 1) * P)
                for k in range(k0, k1):
                    w = slice(k * P, (k + 1) * P)
                    if kind == "x":
                        last = pe.transpose(dst[:, w], xn[:, which, w], ident[:, :])
                    elif kind == "o":
                        par = 1 - blk.batch
                        last = three(dst[:, :], oT_hi[:, par, k, tok], oT_lo[:, par, k, tok], wo_hi[:, k, :],
                                     wo_lo[:, k, :], k == 0, k == KC - 1)
                    else:
                        last = three(dst[:, :], wq_hi[:, k, tok], wq_lo[:, k, tok], xT_hi[:, k, :], xT_lo[:, k, :],
                                     k == 0, k == KC - 1)
                if k1 == KC:
                    last.then_inc(job_done, 1)

            def scores(blk, u):
                c, t = divmod(u, TILES)
                wait(pe, masked, blk.at(UNITS, u - 1))
                if t == 0:
                    pe.wait_ge(job_out, blk.q_ready(c))
                tok = slice(t * P, (t + 1) * P)
                three(S_BANK[u % 2][:, :], qT_hi[:, c % 2, tok], qT_lo[:, c % 2, tok],
                      kbd_hi[:, blk.batch, c, :], kbd_lo[:, blk.batch, c, :], True, True).then_inc(scored, 1)

            def turn(blk, u):
                t = u % TILES
                pe.wait_ge(scaled, blk.at(UNITS, u + 1))
                wait(pe, pT_ready, blk.at(UNITS, u - 1))
                for j in range(4):
                    last = pe.transpose(T_BANK[u % 2][:, j * P:(j + 1) * P], pr[:, t, j, :], ident[:, :])
                last.then_inc(turned, 1)

            def p_v(blk, c):
                if blk.first:
                    slot = next(u for u in PV_SLOTS if PV_SLOTS[u] == c)
                    pe.wait_ge(v_ready, sum(u < slot for u in V_SLOTS))
                pe.wait_ge(pT_ready, blk.at(UNITS, TILES * (c + 1)))
                wait(pe, oT_ready, blk.at(GROUPS, c))
                for j in range(4):
                    h = 4 * c + j
                    last = pe.matmul(PV_BANK[j * DK:(j + 1) * DK, :], v_sb[:, blk.batch, h * DK:(h + 1) * DK],
                                     pT[:, c % 2, j, :], start=True, stop=True)
                last.then_inc(pv_done, 1)

            def v_product(b):
                if b == 0:
                    pe.wait_ge(k_ready, GROUPS)
                else:
                    v_slot = next(u for u in V_SLOTS if V_SLOTS[u] == b)
                    pe.wait_ge(oT_ready, sum(u < v_slot and PV_SLOTS[u] < GROUPS - 1 for u in PV_SLOTS))
                for k in range(KC):
                    last = pe.matmul(PV_BANK[:, :], ctx_raw[:, k, b * KEYS:(b + 1) * KEYS], wv_raw[:, k, :],
                                     start=(k == 0), stop=(k == KC - 1))
                last.then_inc(v_done, 1)

            pe.wait_ge(made, 1)
            for _ in range(WARM_UP):
                pe.transpose(JOB_BANK[2][:, 0:P], ident[:, :], ident[:, :])

            def k_product(c):
                for k in range(KC):
                    last = pe.matmul(K_BANK[c][:, 0:B * KEYS], wk_raw[:, k, c * P:(c + 1) * P], ctx_raw[:, k, :],
                                     start=(k == 0), stop=(k == KC - 1))
                last.then_inc(k_done, 1)

            for t in range(TILES):
                job_steps(t, JOB_BANK[t % 3], t - 2, "x", t, 0, KC, ready=t + 1)
            pe.wait_ge(in_k, 32)
            k_product(0)
            k_product(1)
            pe.wait_ge(wq_ready, KC // 2)
            pe.wait_ge(wq_split, KC)
            pe.wait_ge(job_out, TILES)
            job_steps(TILES, JOB_BANK[TILES % 3], TILES - 2, "q0", 0, 0, KC)
            k_product(2)
            pe.wait_ge(k_ready, 2)

            def attention(blk):
                for u in range(UNITS):
                    if blk.first and u % TILES == 0:
                        pe.wait_ge(kbd_ready, 4 * (u // TILES + 1))
                    scores(blk, u)
                    if blk.first and u == LAG:
                        pe.wait_ge(k_ready, GROUPS - 1)
                    if not (blk.first and u < LAG):
                        turn(*blk.unit(u - LAG))
                    for kind, which, k0, k1 in STEPS[u]:
                        if not blk.has(kind) or blk.held(kind, which):
                            continue
                        if kind == "o":
                            pe.wait_ge(oT_ready, blk.at(GROUPS, k1 - GROUPS))
                            if k0 == 0 and blk.b == 1 and blk.prev().first:
                                pe.wait_ge(wo_step, 2 * KC)
                        if k0 == 0 and kind == "q0":
                            pe.wait_ge(job_out, blk.job("x", TILES - 1) + 1)
                        job = blk.job(kind, which)
                        job_steps(job, JOB_BANK[blk.bank(kind, which)], job - 2, kind, which, k0, k1, blk,
                                  blk.at(TILES, TILES + which + 1))
                    if blk.first and u in K_SLOTS:
                        k_product(K_SLOTS[u])
                    if blk.first and u in V_SLOTS:
                        if u == min(V_SLOTS):
                            pe.wait_ge(in_v, 16)
                        v_product(V_SLOTS[u])
                    if blk.pv(u):
                        p_v(*blk.pv(u))

            all_pairs(pe, attention)

            def up(n, m):
                g = n * MC + m
                wait(pe, relued, g - 1)
                pe.wait_ge(w_step, 4 * m + 2)
                for k in range(KC):
                    w = slice(k * P, (k + 1) * P)
                    last = three(UP_BANK[m % 2][:, :], w_chunk[m][:, 0, w], w_chunk[m][:, 1, w],
                                 xT_hi[:, k, :], xT_lo[:, k, :], k == 0, k == KC - 1)
                last.then_inc(up_done, 1)

            def down(n, m):
                pe.wait_ge(h_ready, n * MC + (m + 1))
                pe.wait_ge(w_step, 4 * m + 4)
                for t in range(TILES):
                    if m == 0 and t == TILES - 1 and isinstance(n, int) and n == 0:
                        pe.wait_ge(job_out, FFN_JOB)
                    if m == 0:
                        wait(pe, summed, n * TILES + (t + 1 - TILES))
                    tok = slice(t * P, (t + 1) * P)
                    three(ACC_BANK[t][:, :], h_hi[:, m % 2, tok], h_lo[:, m % 2, tok], w_chunk[m][:, 2, :],
                          w_chunk[m][:, 3, :], m == 0, m == MC - 1).then_inc(down_done, 1)

            def feed_forward(n, last_block=False, begun=0):
                for m in range(MC):
                    if m >= begun:
                        up(n, m)
                    if 0 < m < MC - 1:
                        down(n, m - 1)
                for t in range(TILES):
                    if not last_block:
                        job_steps(n * TILES + (FFN_JOB + t), TURN_BANK[t % 2],
                                  n * TILES + (FFN_JOB + (0 if t < 2 else t - 1)), "x", t, 0, KC,
                                  ready=n * TILES + (TILES * (NB + 1) + t + 1))
                    if t == 1:
                        down(n, MC - 2)
                down(n, MC - 1)
                if not last_block:
                    pe.wait_ge(job_out, n * TILES + (FFN_JOB + TILES))

            end = Block(PAIRS, 0)
            turn(*end.unit(-3))
            pe.wait_ge(masked, UNITS * NB - 1)
            pe.wait_ge(job_out, end.prev().job("x", TILES - 1) + 1)
            up(0, 0)
            turn(*end.unit(-2))
            pe.wait_ge(masked, UNITS * NB)
            up(0, 1)
            turn(*end.unit(-1))
            p_v(end.prev(), GROUPS - 1)
            job_steps(O_LAST - 1, JOB_BANK[(O_LAST - 1) % 3], O_LAST - 3, "o", TILES - 1, 0, KC, end.prev())
            pe.wait_ge(oT_ready, GROUPS * NB)
            for t in range(TILES):
                job_steps(O_LAST + t, JOB_BANK[(O_LAST + t) % 3], O_LAST + t - 2, "o", t, 0, KC, end)
            pe.wait_ge(pT_ready, UNITS * NB)
            feed_forward(0, begun=2)
            with pe.Fori(1, NB - 1) as n:
                feed_forward(n)
            feed_forward(NB - 1, last_block=True)

        @block.scalar
        def _(act):
            act.dma_start(bk_col[:], bk).then_inc(in_cols, 16)
            act.dma_start(bq_col[:], bq).then_inc(in_cols, 16)
            act.dma_start(b1_col[:], b1).then_inc(in_cols, 16)

            def x_hi(job, src, t):
                act.wait_ge(job_done, job + 1)
                act.activation(xT_hi[:, :, t * P:(t + 1) * P], src[:, :].rearrange("p (k j) -> p k j", j=P),
                               ACT.Copy).then_inc(job_hi, 1)

            def q_hi(job, src, c, units):
                act.wait_ge(job_done, job + 1)
                wait(act, scored, units)
                act.activation(qT_hi[:, c % 2, :], src[:, :], ACT.Identity,
                               bias=bq_col[:, c:c + 1]).then_inc(job_hi, 1)

            def pT_out(blk, u):
                c, t = divmod(u, TILES)
                act.wait_ge(turned, blk.at(UNITS, u + 1))
                if t == 0:
                    wait(act, pv_done, blk.at(GROUPS, c - 1))
                    if blk.first and c == 0:
                        act.wait_ge(k_done, GROUPS)
                act.activation(pT[:, c % 2, :, t * P:(t + 1) * P],
                               T_BANK[u % 2][:, :].rearrange("p (h j) -> p h j", j=P), ACT.Copy).then_inc(pT_ready, 1)

            def exps(blk, u):
                t = u % TILES
                act.wait_ge(maxed, blk.at(UNITS, u + 1))
                wait(act, turned, blk.at(UNITS, u - 3))
                for j in range(4):
                    last = act.activation(pr[:, t, j, :], sc[:, t, j, :], ACT.Exp, bias=neg_max[:, t, j:j + 1],
                                          accum_out=row_sum[:, t, j:j + 1])
                last.then_inc(exped, 1)

            def oT_out(blk, c):
                act.wait_ge(pv_done, blk.at(GROUPS, c + 1))
                if blk.b == 1 and blk.prev().first and c == 0:
                    act.wait_ge(v_ready, B)
                    act.wait_ge(kbd_ready, 4 * GROUPS)
                act.activation(oT_hi[:, blk.batch, c, :], PV_BANK[:, :], ACT.Copy).then_inc(oT_hi_done, 1)

            for t in range(TILES):
                x_hi(t, JOB_BANK[t % 3], t)
            act.wait_ge(in_wq, 16)
            for k in range(KC // 2):
                act.activation(wq_hi[:, k, :], wq_raw[:, k, :], ACT.Copy).then_inc(wq_hi_done, 1)
            act.wait_ge(made, 3)
            act.wait_ge(k_ready, 1)
            for j in range(4):
                act.activation(head(kbd_hi, j, 0), k_head(j, 0), ACT.Copy).then_inc(kbd_first_hi, 1)
            act.wait_ge(in_cols, 48)
            q_hi(TILES, JOB_BANK[TILES % 3], 0, 0)

            def attention(blk):
                for u in range(UNITS):
                    if not (blk.first and u < LAG):
                        pT_out(*blk.unit(u - LAG))
                    exps(blk, u)
                    for kind, which, job, _, n in blk.jobs(u):
                        if kind == "x":
                            x_hi(job, JOB_BANK[n], which)
                        elif kind == "q":
                            q_hi(job, JOB_BANK[n], which, blk.at(UNITS, TILES * (which - 1)))
                        elif kind == "q0":
                            q_hi(job, JOB_BANK[n], 0, blk.at(UNITS, TILES * (GROUPS - 1)))
                    if blk.pv(u):
                        oT_out(*blk.pv(u))

            all_pairs(act, attention)
            end = Block(PAIRS, 0)
            for u in range(-LAG, 0):
                pT_out(*end.unit(u))
            oT_out(end.prev(), GROUPS - 1)

            def feed_forward(n, last_block=False):
                for m in range(MC):
                    g = n * MC + m
                    act.wait_ge(up_done, g + 1)
                    wait(act, h_ready, g - 1)
                    act.activation(h_raw[:, m % 2, :], UP_BANK[m % 2][:, :], ACT.Relu,
                                   bias=b1_col[:, m:m + 1]).then_inc(relued, 1)
                if not last_block:
                    for t in range(TILES):
                        x_hi(n * TILES + (FFN_JOB + t), TURN_BANK[t % 2], t)

            feed_forward(0)
            with act.Fori(1, NB - 1) as n:
                feed_forward(n)
            feed_forward(NB - 1, last_block=True)

        @block.vector
        def _(dve):
            def count(t, ready):
                dve.wait_ge(in_x[t], ready)
                dve.bn_stats(stats[:, t, :], xn[:, t, :]).then_inc(counted, 1)

            def mean(done, t):
                dve.wait_ge(counted, done + 1)
                wait(dve, normed, done - t)
                dve.sem_inc(passed, 1)
                dve.bn_aggr(mean_var[:, t, :], stats[:, t, :]).then_inc(meaned, 1)

            def normalise(t, ready):
                dve.wait_ge(rstd_ready, ready)
                dve.tensor_scalar(xn[:, t, :], xn[:, t, :], mean_var[:, t, 0:1], rstd[:, t:t + 1],
                                  ALU.subtract, ALU.mult).then_inc(normed, 1)

            def x_lo(hi_no, src, t):
                dve.wait_ge(job_hi, hi_no + 1)
                tok = slice(t * P, (t + 1) * P)
                dve.tensor_tensor(xT_lo[:, :, tok], src[:, :].rearrange("p (k j) -> p k j", j=P),
                                  xT_hi[:, :, tok].bitcast(F32), ALU.subtract).then_inc(job_out, 1)

            def q_lo(hi_no, src, c):
                dve.wait_ge(job_hi, hi_no + 1)
                dve.scalar_tensor_tensor(out=qT_lo[:, c % 2, :], in0=src[:, :], scalar=bq_col[:, c:c + 1],
                                         in1=qT_hi[:, c % 2, :].bitcast(F32), op0=ALU.add,
                                         op1=ALU.subtract).then_inc(job_out, 1)

            def x2_sum(job, src, t, ready):
                dve.wait_ge(job_done, job + 1)
                dve.wait_ge(biased, ready)
                dve.tensor_tensor(res[:, t, :], src[:, :], res[:, t, :], ALU.add).then_inc(job_out, 1)

            def oT_low(blk, c):
                dve.wait_ge(oT_hi_done, blk.at(GROUPS, c + 1))
                dve.tensor_tensor(oT_lo[:, blk.batch, c, :], PV_BANK[:, :],
                                  oT_hi[:, blk.batch, c, :].bitcast(F32), ALU.subtract).then_inc(oT_ready, 1)

            for t in range(TILES):
                count(t, 16)
                mean(t, t)
            dve.wait_ge(in_cols, 48)

            def k_out(c):
                dve.wait_ge(k_done, c + 1)
                dve.tensor_scalar(k_raw[:, c], K_BANK[c][:, 0:B * KEYS].rearrange("p (b k) -> p b k", b=B),
                                  bk_col[:, c:c + 1], float(DK) ** -0.5, ALU.add, ALU.mult).then_inc(k_ready, 1)

            def kbd_low(c):
                for j in range(4):
                    if c == 0:
                        dve.wait_ge(kbd_first_hi, j + 1)
                    else:
                        dve.wait_ge(kbd_hi_done, 4 * (c - 1) + j + 1)
                    dve.tensor_tensor(head(kbd_lo, j, c), k_head(j, c), head(kbd_hi, j, c).bitcast(F32),
                                      ALU.subtract).then_inc(kbd_ready, 1)

            for t in range(TILES):
                normalise(t, 1)
            for t in range(TILES):
                x_lo(t, JOB_BANK[t % 3], t)
            k_out(0)
            for k in range(KC // 2):
                dve.wait_ge(wq_hi_done, k + 1)
                dve.tensor_tensor(wq_lo[:, k, :], wq_raw[:, k, :], wq_hi[:, k, :].bitcast(F32),
                                  ALU.subtract).then_inc(wq_ready, 1)
            kbd_low(0)
            k_out(1)
            q_lo(TILES, JOB_BANK[TILES % 3], 0)

            def v_out(b):
                if b == 0:
                    dve.wait_ge(in_bv, 16)
                dve.wait_ge(v_done, b + 1)
                dve.tensor_tensor(v_sb[:, b, :], PV_BANK[:, :], bv_row[:], ALU.add).then_inc(v_ready, 1)

            def late(blk, u):
                for kind, which, job, hi_no, n in blk.jobs(u):
                    if blk.held(kind, which):
                        continue
                    if kind == "x":
                        x_lo(hi_no, JOB_BANK[n], which)
                    elif kind == "o":
                        x2_sum(job, JOB_BANK[n], which, blk.at(TILES, which + 1 - TILES))
                    else:
                        q_lo(hi_no, JOB_BANK[n], which)
                if blk.first and u in K_OUT_SLOTS:
                    k_out(K_OUT_SLOTS[u])
                if blk.first and u in V_SLOTS:
                    v_out(V_SLOTS[u])
                if blk.pv(u):
                    oT_low(*blk.pv(u))

            def invert(blk, u):
                t = u % TILES
                dve.wait_ge(exped, blk.at(UNITS, u + 1))
                wait(dve, scaled, blk.at(UNITS, u - 3))
                dve.reciprocal(row_inv[:, t, :], row_sum[:, t, :]).then_inc(inverted, 1)

            def attention(blk):
                for u in range(UNITS):
                    c, t = divmod(u, TILES)
                    dve.wait_ge(scored, blk.at(UNITS, u + 1))
                    wait(dve, exped, blk.at(UNITS, u - 3))
                    if c == 0:
                        dve.wait_ge(filled, blk.at(TILES, t + 1))
                    if u == 0:
                        dve.wait_ge(in_mask[blk.b], blk.i * 16 + 16)
                    dve.sem_inc(passed, 1)
                    dve.copy_predicated(sc[:, t], mask_sb[:, blk.b, t, :].unsqueeze(1).to_broadcast([P, 4, KEYS]),
                                        S_BANK[u % 2][:, :].rearrange("p (h k) -> p h k", k=KEYS)).then_inc(masked, 1)
                    if u in STATS_SLOTS:
                        count(STATS_SLOTS[u], blk.at(16, 32))
                    if not (blk.first and u == 0):
                        invert(*blk.unit(u - 1))
                    dve.wait_ge(masked, blk.at(UNITS, u + 1))
                    dve.tensor_reduce(neg_max[:, t, :], sc[:, t], AX.X, ALU.max, negate=True).then_inc(maxed, 1)
                    if u in STATS_SLOTS:
                        mean(blk.at(TILES, TILES + STATS_SLOTS[u]), STATS_SLOTS[u])
                    if not (blk.first and u == 0):
                        late(*blk.unit(u - 1))
                    if blk.first and u in KBD_LOW_SLOTS:
                        kbd_low(KBD_LOW_SLOTS[u])
                    if u in APPLY_SLOTS:
                        normalise(APPLY_SLOTS[u], blk.at(1, 2))

            all_pairs(dve, attention)
            end = Block(PAIRS, 0)
            invert(*end.unit(-1))
            late(Block(PAIRS - 1, 1, last=True), UNITS - 1)
            oT_low(end.prev(), GROUPS - 1)

            def h_hi_out(g, m):
                dve.wait_ge(relued, g + 1)
                wait(dve, down_done, g * TILES - TILES)
                dve.tensor_copy(h_hi[:, m % 2, :], h_raw[:, m % 2, :]).then_inc(hi_done, 1)

            def h_lo_out(g, m):
                dve.wait_ge(hi_done, g + 1)
                dve.tensor_tensor(h_lo[:, m % 2, :], h_raw[:, m % 2, :], h_hi[:, m % 2, :].bitcast(F32),
                                  ALU.subtract).then_inc(h_ready, 1)

            x2_sum(O_LAST - 1, JOB_BANK[(O_LAST - 1) % 3], TILES - 1, TILES * (NB - 1))
            h_hi_out(0, 0)
            h_lo_out(0, 0)
            for t in range(TILES):
                x2_sum(O_LAST + t, JOB_BANK[(O_LAST + t) % 3], t, TILES * (NB - 1) + t + 1)

            def feed_forward(n, last_block=False, begun=0):
                for m in range(begun, MC):
                    g = n * MC + m
                    h_hi_out(g, m)
                    if 2 <= m < 2 + TILES and not last_block:
                        count(m - 2, n * 16 + 16 * (NB + 2))
                    h_lo_out(g, m)
                    if 2 <= m < 2 + TILES and not last_block:
                        mean(n * TILES + (TILES * (NB + 1) + m - 2), m - 2)
                    if MC - 1 - TILES <= m < MC - 1 and not last_block:
                        normalise(m - (MC - 1 - TILES), n + (NB + 2))
                if not last_block:
                    for t in range(TILES):
                        x_lo(n * TILES + (FFN_HI + t), TURN_BANK[t % 2], t)
                for t in range(TILES):
                    dve.wait_ge(down_done, n * (MC * TILES) + ((MC - 1) * TILES + t + 1))
                    dve.wait_ge(biased, n * TILES + (TILES * NB + t + 1))
                    dve.tensor_tensor(res[:, t, :], ACC_BANK[t][:, :], res[:, t, :], ALU.add).then_inc(summed, 1)

            feed_forward(0, begun=1)
            with dve.Fori(1, NB - 1) as n:
                feed_forward(n)
            feed_forward(NB - 1, last_block=True)

        @block.gpsimd
        def _(pool):
            def split(raw, hi, lo, sem_, before):
                pool.tensor_scalar(hi, raw, 1.0, 0.0, ALU.mult, ALU.add).then_inc(sem_, 1)
                pool.wait_ge(sem_, before + 1)
                pool.tensor_tensor(lo, raw, hi.bitcast(F32), ALU.subtract).then_inc(sem_, 1)

            def rstds(ready):
                pool.wait_ge(meaned, ready * TILES)
                pool.tensor_tensor(rstd[:], mean_var[:, :, 1], eps[:], ALU.add).then_inc(eps_added, 1)
                pool.wait_ge(eps_added, ready)
                pool.tensor_tensor(rstd[:], rstd[:], minus_half[:], ALU.pow).then_inc(rstd_ready, 1)

            def add_bias(t, landed, row):
                pool.wait_ge(in_res[t], landed)
                pool.tensor_tensor(res[:, t, :], res[:, t, :], row[:], ALU.add).then_inc(biased, 1)

            def fill(t):
                pool.memset(sc[:, t], MASKED).then_inc(filled, 1)

            def scale(blk, u):
                t = u % TILES
                pool.wait_ge(inverted, blk.at(UNITS, u + 1))
                pool.tensor_tensor(pr[:, t], pr[:, t], row_inv[:, t, :].unsqueeze(2).to_broadcast([P, 4, KEYS]),
                                   ALU.mult).then_inc(scaled, 1)

            def make_weights(first, end):
                for part in range(first, end):
                    m, kind = divmod(part, 4)
                    raw = w_stage[:, m % STAGE, kind // 2, :]
                    if kind % 2 == 0:
                        pool.wait_ge(in_w[m % STAGE], 32 * (m // STAGE + 1))
                        pool.tensor_scalar(w_chunk[m][:, kind, :], raw, 1.0, 0.0, ALU.mult,
                                           ALU.add).then_inc(w_step, 1)
                    else:
                        pool.wait_ge(w_step, part)
                        pool.tensor_tensor(w_chunk[m][:, kind, :], raw, w_chunk[m][:, kind - 1, :].bitcast(F32),
                                           ALU.subtract).then_inc(w_step, 1)

            pool.memset(minus_half[:], -0.5).then_inc(zeroed, 1)
            pool.memset(eps[:], EPS).then_inc(zeroed, 1)
            pool.memset(ident[:], 0.0).then_inc(zeroed, 1)
            pool.wait_ge(zeroed, 3)
            pool.affine_select(out=ident[:], in_=ident[:], compare_op=ALU.not_equal, fill=1.0, base=0,
                               pattern=[[-1, P]], channel_multiplier=1).then_inc(made, 1)
            pool.memset(kbd_hi[:].bitcast(F32), 0.0).then_inc(made, 1)
            for t in range(TILES):
                fill(t)
            rstds(1)
            pool.memset(kbd_lo[:].bitcast(F32), 0.0).then_inc(made, 1)

            def kbd_high(c):
                pool.wait_ge(k_ready, c + 1)
                for j in range(4):
                    if j > 0:
                        pool.wait_ge(kbd_hi_done, 4 * (c - 1) + j)
                    pool.tensor_scalar(head(kbd_hi, j, c), k_head(j, c), 1.0, 0.0, ALU.mult,
                                       ALU.add).then_inc(kbd_hi_done, 1)
                pool.wait_ge(kbd_hi_done, 4 * c)

            pool.wait_ge(in_wq, 16)
            for k in range(KC // 2, KC):
                split(wq_raw[:, k, :], wq_hi[:, k, :], wq_lo[:, k, :], wq_split, 2 * (k - KC // 2))
            pool.wait_ge(wq_split, KC)
            kbd_high(1)

            def attention(blk):
                for u in range(UNITS):
                    if not (blk.first and u == 0):
                        scale(*blk.unit(u - 1))
                    if blk.first and u in KBD_HI_SLOTS:
                        pool.wait_ge(scaled, u)
                        kbd_high(KBD_HI_SLOTS[u])
                    if blk.first and u in WO_SLOTS:
                        k, low = divmod(WO_SLOTS[u], 2)
                        if low:
                            pool.wait_ge(wo_step, 2 * k + 1)
                            pool.tensor_tensor(wo_lo[:, k, :], wo_raw[:, k, :], wo_hi[:, k, :].bitcast(F32),
                                               ALU.subtract).then_inc(wo_step, 1)
                        else:
                            if k == 0:
                                pool.wait_ge(in_wo, 16)
                            pool.tensor_scalar(wo_hi[:, k, :], wo_raw[:, k, :], 1.0, 0.0, ALU.mult,
                                               ALU.add).then_inc(wo_step, 1)
                    if u > UNITS - TILES and not blk.last:
                        fill(u - 1 - (UNITS - TILES))
                    if u == 0 and not blk.first:
                        fill(TILES - 1)
                    if blk.last and u in W_SLOTS:
                        if u == min(W_SLOTS):
                            pool.wait_ge(job_done, blk.job("q", GROUPS - 1) + 1)
                        make_weights(W_SLOTS[u], W_SLOTS[u] + 1)
                    if u == RSTD_SLOT:
                        rstds(blk.at(1, 2))
                    if u == min(BIAS_SLOTS) and blk.b == 1 and blk.prev().first:
                        pool.wait_ge(in_rows, 32)
                    if u in BIAS_SLOTS and not blk.first:
                        add_bias(BIAS_SLOTS[u], blk.at(16), bo_row)

            all_pairs(pool, attention)
            scale(*Block(PAIRS, 0).unit(-1))
            made_parts = len(W_SLOTS)
            make_weights(made_parts, 4 * q_chunks)
            for t in range(TILES - 1):
                add_bias(t, 16 * NB, bo_row)
            pool.wait_ge(scored, UNITS * NB)
            make_weights(4 * q_chunks, 4 * q_chunks + 4)
            add_bias(TILES - 1, 16 * NB, bo_row)
            make_weights(4 * q_chunks + 4, 4 * early_chunks)
            pool.wait_ge(job_done, FFN_JOB)
            make_weights(4 * early_chunks, 4 * MC)

            def feed_forward(n, last_block=False):
                for t in range(TILES):
                    add_bias(t, n * 16 + 16 * (NB + 1), b2_row)
                if not last_block:
                    rstds(n + (NB + 2))

            feed_forward(0)
            with pool.Fori(1, NB - 1) as n:
                feed_forward(n)
            feed_forward(NB - 1, last_block=True)


def kernel(x, ctx_1024, mask_Bx1xSxS2_ik0, L0_xattn_Wq, L0_xattn_bq, L0_xattn_Wk, L0_xattn_bk, L0_xattn_Wv,
           L0_xattn_bv, L0_xattn_Wo, L0_xattn_bo, L0_ffn_W1, L0_ffn_b1, L0_ffn_W2, L0_ffn_b2):
    import numpy as np
    import concourse.bacc as bacc
    from concourse.bass_utils import run_bass_kernel_spmd

    lay = np.ascontiguousarray
    x, ctx, mask = np.asarray(x), np.asarray(ctx_1024), np.asarray(mask_Bx1xSxS2_ik0)
    arrays = {
        "x": lay(x.reshape(B * S, D)),
        "ctxT": lay(ctx.reshape(B * KEYS, D).T),
        "mask": lay(mask.reshape(B * S, KEYS)),
        "wqT": lay(np.asarray(L0_xattn_Wq).T), "bq": lay(np.asarray(L0_xattn_bq).reshape(KC, P).T),
        "wkT": lay(np.asarray(L0_xattn_Wk).T), "bk": lay(np.asarray(L0_xattn_bk).reshape(KC, P).T),
        "wvT": lay(np.asarray(L0_xattn_Wv).T), "bv": lay(np.asarray(L0_xattn_bv).reshape(1, D)),
        "woT": lay(np.asarray(L0_xattn_Wo).T), "bo": lay(np.asarray(L0_xattn_bo).reshape(1, D)),
        "w1": lay(np.asarray(L0_ffn_W1)), "b1": lay(np.asarray(L0_ffn_b1).reshape(MC, P).T),
        "w2": lay(np.asarray(L0_ffn_W2)), "b2": lay(np.asarray(L0_ffn_b2).reshape(1, D)),
    }
    nc = bacc.Bacc("TRN2", target_bir_lowering=False, num_devices=1)
    args = [nc.dram_tensor(f"in_{name}", a.shape, mybir.dt.from_np(a.dtype), kind="ExternalInput").ap()
            for name, a in arrays.items()]
    x2 = nc.dram_tensor("x2_between", (B * S, D), F32, kind="Internal").ap()
    out = nc.dram_tensor("out_0", (B * S, D), F32, kind="ExternalOutput").ap()
    build(nc, *args, x2, out)
    r = run_bass_kernel_spmd(nc, [{f"in_{name}": a for name, a in arrays.items()}], core_ids=[0])
    return r.results[0]["out_0"].reshape(B, S, D)
```
